# Optimizing a Trainium2 kernel written in Bass

```python
import numpy as np
import jax
import jax.numpy as jnp

def _softmax(x, axis=-1):
    return jax.nn.softmax(x, axis=axis)

def _gelu(x):
    return jax.nn.gelu(x, approximate=True)

def _silu(x):
    return jax.nn.silu(x)

def _sigmoid(x):
    return jax.nn.sigmoid(x)

def _layernorm(x, axis=-1, eps=1e-05):
    m = jnp.mean(x, axis=axis, keepdims=True)
    v = jnp.var(x, axis=axis, keepdims=True)
    return (x - m) / jnp.sqrt(v + eps)

def _scatter_add(tgt, idx, src, axis=0):
    return tgt.at[idx].add(src)

def _segment_sum(src, seg, n):
    return jax.ops.segment_sum(src, seg, n)
kernel_name = 'mk_gnn_resnorm_d1_gnn_r8_ef6d66'

def setup_inputs(seed: int=0):
    np.random.seed(seed)
    _w = jnp.asarray

    def _rec_inputs():
        import jax
        import jax.numpy as jnp
        _gk = jax.random.key(seed)
        x = -0.0006008 + 1.001 * jax.random.normal(jax.random.fold_in(_gk, 1), (6250, 256), jnp.float32)
        _s = jax.random.randint(jax.random.fold_in(_gk, 2), (50000,), 0, 6250, jnp.int32)
        _d = jax.random.randint(jax.random.fold_in(_gk, 3), (50000,), 0, 6250, jnp.int32)
        _loop = jnp.arange(6250, dtype=jnp.int32)
        src = jnp.concatenate([_s, _d, _loop])
        dst = jnp.concatenate([_d, _s, _loop])
        _o = jnp.argsort(dst, stable=True)
        src = src[_o]
        dst = dst[_o]
        edge_attr_64 = 0.000312547 + 1.00004 * jax.random.normal(jax.random.fold_in(_gk, 11), (106250, 64), jnp.float32)
        return (x, src, dst, edge_attr_64)
    x, src, dst, edge_attr_64 = _rec_inputs()

    def _L0_gnn_setup():
        import jax, jax.numpy as jnp
        import numpy as np
        N, E, H, DE = (1250, 31250, 256, 64)
        EPS = 1e-05

        def _lin_init(k, fan_in, shape):
            s = 1.0 / np.sqrt(fan_in)
            return jax.random.uniform(k, shape, jnp.float32, -s, s)
        key = jax.random.key(seed)
        ks = jax.random.split(key, 12)
        x = jax.random.normal(ks[0], (N, H), jnp.float32)
        edge_index = jax.random.randint(ks[1], (2, E), 0, N)
        edge_attr = jax.random.normal(ks[2], (E, DE), jnp.float32)
        d_in = H + DE
        W1 = _lin_init(ks[3], d_in, (d_in, H))
        b1 = _lin_init(ks[4], d_in, (H,))
        W2 = _lin_init(ks[5], H, (H, H))
        b2 = _lin_init(ks[6], H, (H,))
        Wg = _lin_init(ks[7], d_in, (d_in, H))
        bg = _lin_init(ks[8], d_in, (H,))
        gamma = jnp.ones((H,), jnp.float32)
        beta = jnp.zeros((H,), jnp.float32)
        return {'x': x, 'edge_index': edge_index, 'edge_attr': edge_attr, 'W1': W1, 'b1': b1, 'W2': W2, 'b2': b2, 'Wg': Wg, 'bg': bg, 'gamma': gamma, 'beta': beta}
    _L0_gnn_all = _L0_gnn_setup()
    _L0_gnn_in = {k: v for k, v in _L0_gnn_all.items() if k in ('W1', 'b1', 'W2', 'b2', 'Wg', 'bg', 'gamma', 'beta')}
    del _L0_gnn_all
    return {'x': x, 'src': src, 'dst': dst, 'edge_attr_64': edge_attr_64, 'L0_gnn_W1': _L0_gnn_in['W1'], 'L0_gnn_b1': _L0_gnn_in['b1'], 'L0_gnn_W2': _L0_gnn_in['W2'], 'L0_gnn_b2': _L0_gnn_in['b2'], 'L0_gnn_Wg': _L0_gnn_in['Wg'], 'L0_gnn_bg': _L0_gnn_in['bg'], 'L0_gnn_gamma': _L0_gnn_in['gamma'], 'L0_gnn_beta': _L0_gnn_in['beta']}

def reference(x, src, dst, edge_attr_64, L0_gnn_W1, L0_gnn_b1, L0_gnn_W2, L0_gnn_b2, L0_gnn_Wg, L0_gnn_bg, L0_gnn_gamma, L0_gnn_beta):
    import jax
    import jax.numpy as jnp

    def _L0_gnn_ref(x, edge_index, edge_attr, W1, b1, W2, b2, Wg, bg, gamma, beta):
        import jax, jax.numpy as jnp
        import numpy as np
        N, E, H, DE = (1250, 31250, 256, 64)
        EPS = 1e-05

        def _lin_init(k, fan_in, shape):
            s = 1.0 / np.sqrt(fan_in)
            return jax.random.uniform(k, shape, jnp.float32, -s, s)
        src, dst = (edge_index[0], edge_index[1])
        ei = jnp.concatenate([x[src], edge_attr], axis=-1)
        core = jnp.maximum(ei @ W1 + b1, 0.0) @ W2 + b2
        gate = jax.nn.sigmoid(ei @ Wg + bg)
        msg = gate * core
        agg = jax.ops.segment_sum(msg, dst, num_segments=x.shape[0])
        out = agg + x
        mu = jnp.mean(out, axis=-1, keepdims=True)
        var = jnp.var(out, axis=-1, keepdims=True)
        out = (out - mu) * jax.lax.rsqrt(var + EPS) * gamma + beta
        return out
    edge_index = jnp.stack([src, dst])
    x = _layernorm(x + _L0_gnn_ref(x, edge_index, edge_attr_64, L0_gnn_W1, L0_gnn_b1, L0_gnn_W2, L0_gnn_b2, L0_gnn_Wg, L0_gnn_bg, L0_gnn_gamma, L0_gnn_beta), axis=-1)
    return x

_drawn_inputs = setup_inputs


def setup_inputs(seed=0):
    import zlib

    import numpy as np

    out = dict(_drawn_inputs(seed))
    spreads = {'L0_gnn_gamma': (1.0, 0.2), 'L0_gnn_beta': (0.0, 0.1)}
    factors = {'L0_gnn_bg': 8.0}
    for name, (base, spread) in spreads.items():
        noise = np.random.default_rng([zlib.crc32(name.encode()), seed]).standard_normal(out[name].shape)
        drawn = base * np.exp(spread * noise) if base else spread * noise
        out[name] = jnp.asarray(drawn.astype(out[name].dtype))
    for name, factor in factors.items():
        out[name] = (out[name] * factor).astype(out[name].dtype)
    return out
```

```python
from contextlib import ExitStack

import concourse.bass as bass
from concourse import mybir

F32 = mybir.dt.float32
F32R = mybir.dt.float32r
I32 = mybir.dt.int32
ALU = mybir.AluOpType
ACT = mybir.ActivationFunctionType
AX_X = mybir.AxisListType.X

P = 128
N, H, DE, E = 6250, 256, 64, 106250
EPS = 1e-5
TPG = 8
PPG = TPG // 2
GROUPS = -(-E // (TPG * P))
TILES = GROUPS * TPG
PAIRS = GROUPS * PPG
GE = TPG * P
HALF = GE // 2
WIN = P
SUM_ROWS = -(-(N + WIN) // P) * P
NT = -(-N // P)
XC = 7
XCHUNKS = NT // XC
XN = XC * P
NR = 8
NCHUNKS = N // (P * NR)
NREST = N - NCHUNKS * P * NR


def gnn_program(nc, xT, x, src_t, dst_t, dst, eaT, w1, b1, w2, b2, wg, bg, gamma, beta, ident_d, iota_d, out):
    assert NT == XC * XCHUNKS and 0 < NREST <= P
    node_table = nc.dram_tensor("node_table", (N, 2 * H), F32).ap()
    node_sum = nc.dram_tensor("node_sum", (SUM_ROWS, H), F32).ap()
    with ExitStack() as ctx:
        def sb(name, shape, dt=F32):
            return ctx.enter_context(nc.sbuf_tensor(name, shape, dt))

        def sem(name):
            return ctx.enter_context(nc.semaphore(name))

        bank = [ctx.enter_context(nc.psum_tensor(f"bank{i}", [P, 512], F32)) for i in range(8)]
        ps_h = [bank[i][:, :].rearrange("p (c e) -> p c e", c=2) for i in (0, 1)]
        ps_g = [bank[i][:, :].rearrange("p (t f) -> p t f", t=2) for i in (2, 3)]
        ps_c = [bank[i][:, :].rearrange("p (t f) -> p t f", t=2) for i in (4, 5)]
        ps_sum = bank[6][:, 0:H]
        ps_misc = bank[7]

        ident = sb("ident", [P, P])
        iota_row = sb("iota_row", [P, WIN])
        iota_part = sb("iota_part", [P, 1])
        ones = sb("ones", [P, P])
        wtab_raw = sb("wtab_raw", [P, 2, 2 * H])
        wtab_hi = sb("wtab_hi", [P, 2, 2 * H], F32R)
        wtab_lo = sb("wtab_lo", [P, 2, 2 * H], F32R)
        we_raw = sb("we_raw", [P, 2 * H])
        we_hi = sb("we_hi", [P, 2 * H], F32R)
        we_lo = sb("we_lo", [P, 2 * H], F32R)
        w2_raw = sb("w2_raw", [P, 2, H])
        w2_hi = sb("w2_hi", [P, 2, H], F32R)
        w2_lo = sb("w2_lo", [P, 2, H], F32R)
        b2_raw = sb("b2_raw", [P, 2 * H])
        b2_hi = sb("b2_hi", [P, 2 * H], F32R)
        b2_parts = sb("b2_parts", [P, 2 * H], F32R)
        b2_sel = sb("b2_sel", [P, P], F32R)
        bias_tab = sb("bias_tab", [P, 2 * H])
        gamma_b = sb("gamma_b", [P, H])
        beta_b = sb("beta_b", [P, H])
        eps_t = sb("eps_t", [P, 1])

        src_idx = sb("src_idx", [P, TILES], I32)
        dst_i = sb("dst_i", [P, TILES], I32)
        dst_f = sb("dst_f", [P, TILES])
        dst_rel = sb("dst_rel", [P, TILES])
        grp_i = sb("grp_i", [GROUPS, GE], I32)
        grp_f = sb("grp_f", [GROUPS, GE])
        grp_min = sb("grp_min", [GROUPS, 1])
        grp_max = sb("grp_max", [GROUPS, 1])
        grp_span = sb("grp_span", [GROUPS, 1])
        grp_diag = sb("grp_diag", [GROUPS, 2, GROUPS])
        win_base = sb("win_base", [P, GROUPS])
        win_clip = sb("win_clip", [P, GROUPS])
        sum_idx = sb("sum_idx", [P, GROUPS], I32)
        span_max = sb("span_max", [P, 1])
        span_int = sb("span_int", [P, 1], I32)
        more_passes = sb("more_passes", [P, 1], I32)

        gat = sb("gat", [P, TPG, 2 * H])
        gat_idx = sb("gat_idx", [P, TPG], I32)
        sct_idx = sb("sct_idx", [P, 1], I32)
        ea_raw = sb("ea_raw", [DE, 2, HALF])
        ea_st = sb("ea_st", [P, 2, HALF], F32R)
        h_hi = sb("h_hi", [P, 2, 2, 2 * P], F32R)
        h_lo = sb("h_lo", [P, 2, 2, 2 * P], F32R)
        gate = sb("gate", [P, 2, 2, H])
        msg = sb("msg", [P, 2, 2, H])
        m_hi = sb("m_hi", [P, 2, 2, H], F32R)
        m_lo = sb("m_lo", [P, 2, 2, H], F32R)
        sel = sb("sel", [P, PPG, 2, WIN], F32R)
        win_sum = sb("win_sum", [P, H])

        x_raw = sb("x_raw", [P, 2, 2, XN])
        x_hi = sb("x_hi", [P, 2, 2, XN], F32R)
        x_lo = sb("x_lo", [P, 2, 2, XN], F32R)
        tab_out = sb("tab_out", [P, 2, 2 * H])
        zero_rows = sb("zero_rows", [P, H])

        n_sum = sb("n_sum", [P, 2, NR, H])
        n_x = sb("n_x", [P, 2, NR, H])
        n_bn = sb("n_bn", [P, 2, NR, 6])
        n_mv = sb("n_mv", [P, 2, 2, NR, 2])
        n_sd = sb("n_sd", [P, 2, 2, NR])
        n_rs = sb("n_rs", [P, 2, 2, NR])
        n_nm = sb("n_nm", [P, 2, 2, NR])

        consts_set = sem("consts_set")
        consts_loaded = sem("consts_loaded")
        weights_loaded = sem("weights_loaded")
        indices_loaded = sem("indices_loaded")
        w_hi_done = sem("w_hi_done")
        w_lo_done = sem("w_lo_done")
        b2_step = sem("b2_step")
        stat_step = sem("stat_step")
        diag_ready = sem("diag_ready")
        stats_spread = sem("stats_spread")
        passes_known = sem("passes_known")
        windows_set = sem("windows_set")
        windows_moved = sem("windows_moved")
        x_loaded = [sem(f"x_loaded{i}") for i in range(2)]
        x_hi_done = sem("x_hi_done")
        x_lo_done = sem("x_lo_done")
        table_mm = sem("table_mm")
        table_biased = sem("table_biased")
        table_stored = [sem(f"table_stored{i}") for i in range(2)]
        node_sum_set = sem("node_sum_set")
        ea_loaded = [sem(f"ea_loaded{i}") for i in range(2)]
        ea_hi_done = sem("ea_hi_done")
        ea_lo_done = sem("ea_lo_done")
        idx_copied = sem("idx_copied")
        gathered = [sem(f"gathered{i}") for i in range(TPG)]
        h_ready = sem("h_ready")
        g_ready = sem("g_ready")
        hhi_done = sem("hhi_done")
        hlo_done = sem("hlo_done")
        gadd_done = sem("gadd_done")
        gate_done = sem("gate_done")
        core_ready = sem("core_ready")
        msg_done = sem("msg_done")
        mhi_done = sem("mhi_done")
        mlo_done = sem("mlo_done")
        sel_ready = sem("sel_ready")
        seg_done = sem("seg_done")
        sum_copied = sem("sum_copied")
        pool_waited = sem("pool_waited")
        sum_added = sem("sum_added")
        pass_open = sem("pass_open")
        sct_idx_copied = sem("sct_idx_copied")
        n_loaded = [sem(f"n_loaded{i}") for i in range(2)]
        n_bn_done = sem("n_bn_done")
        n_mv_done = sem("n_mv_done")
        n_sd_done = sem("n_sd_done")
        n_rs_done = sem("n_rs_done")
        n_nm_done = sem("n_nm_done")
        n_applied = sem("n_applied")
        n_xb_done = sem("n_xb_done")
        n_scaled = sem("n_scaled")
        n_mid_done = sem("n_mid_done")
        n_stored = [sem(f"n_stored{i}") for i in range(2)]

        xT_v = xT.rearrange("(c p) n -> p c n", c=2)
        W_LOADS = 9
        C_LOADS = 11
        norm_order = [(0, 0)]
        for c in range(NCHUNKS + 1):
            norm_order += [(c + 1, 0)] * (c < NCHUNKS) + [(c, 1)]

        block = ctx.enter_context(nc.Block())

        def passes(eng):
            eng.wait_ge(passes_known, 1)
            return eng.value_load(more_passes[0:1, 0:1], min_val=0, max_val=N // WIN + 1)

        def pass_start(eng, ps):
            eng.wait_ge(pass_open, ps + 1)

        def norm_rows(c):
            first = c * P * NR
            if c < NCHUNKS:
                return P, NR, slice(first, first + P * NR)
            return NREST, 1, slice(first, N)

        @block.sync
        def _(sp):
            sp.dma_start(x_raw[:, 0], xT_v[:, :, 0:XN]).then_inc(x_loaded[0], 16)
            for c in range(2):
                sp.dma_start(wtab_raw[:, c, 0:H], w1[c * P:(c + 1) * P, :]).then_inc(weights_loaded, 16)
                sp.dma_start(wtab_raw[:, c, H:], wg[c * P:(c + 1) * P, :]).then_inc(weights_loaded, 16)
            for k in range(2):
                sp.dma_start(we_raw[k * DE:(k + 1) * DE, 0:H], w1[H:H + DE, :]).then_inc(weights_loaded, 16)
                sp.dma_start(we_raw[k * DE:(k + 1) * DE, H:], wg[H:H + DE, :]).then_inc(weights_loaded, 16)
            sp.dma_start(w2_raw[:], w2.rearrange("(c p) f -> p c f", c=2)).then_inc(weights_loaded, 16)
            sp.dma_start(x_raw[:, 1], xT_v[:, :, XN:2 * XN]).then_inc(x_loaded[1], 16)

            for t in range(NT):
                c, tt = t // XC, t % XC
                if tt == 0 and 1 <= c and c + 1 < XCHUNKS:
                    n = min(XN, N - (c + 1) * XN)
                    sp.wait_ge(x_lo_done, c)
                    sp.dma_start(x_raw[:, (c + 1) % 2, :, 0:n],
                                 xT_v[:, :, (c + 1) * XN:(c + 1) * XN + n]).then_inc(x_loaded[(c + 1) % 2], 16)
                m = min(P, N - t * P)
                sp.wait_ge(table_biased, t + 1)
                sp.dma_start(node_table[t * P:t * P + m, :], tab_out[0:m, t % 2, :]).then_inc(table_stored[t % 2], 16)

            more = passes(sp)
            with sp.Fori(0, more + 1) as ps:
                pass_start(sp, ps)
                for h in range(2):
                    sp.dma_start(ea_raw[:, h, :], eaT[0, :, h * HALF:(h + 1) * HALF]).then_inc(ea_loaded[h], 16)
                with sp.Fori(1, GROUPS) as g:
                    for h in range(2):
                        sp.wait_ge(ea_lo_done, (ps * GROUPS + g) * 2 + (h - 1))
                        sp.dma_start(ea_raw[:, h, :], eaT[bass.ds(g, 1), :, h * HALF:(h + 1) * HALF].rearrange(
                            "o d e -> (o d) e")).then_inc(ea_loaded[h], 16)

            sp.wait_ge(pass_open, more + 2)
            for c in range(NCHUNKS + 1 + 2):
                if c >= 2:
                    q, (rows, R, at) = (c - 2) % 2, norm_rows(c - 2)
                    sp.wait_ge(n_applied, norm_order.index((c - 2, 1)) + 1)
                    sp.dma_start(out[at, :].rearrange("(p r) f -> p r f", r=R), n_sum[0:rows, q, 0:R, :]).then_inc(n_stored[q], 16)
                if c <= NCHUNKS:
                    q, (rows, R, at) = c % 2, norm_rows(c)
                    if c >= 2:
                        sp.wait_ge(n_stored[q], 16 * (c // 2))
                    sp.dma_start(n_sum[0:rows, q, 0:R, :], node_sum[at, :].rearrange("(p r) f -> p r f", r=R)).then_inc(n_loaded[q], 16)
                    sp.dma_start(n_x[0:rows, q, 0:R, :], x[at, :].rearrange("(p r) f -> p r f", r=R)).then_inc(n_loaded[q], 16)
            for q in range(2):
                sp.wait_ge(n_stored[q], 16 * ((NCHUNKS + 1 + 1 - q) // 2))

        @block.scalar
        def _(act):
            rest = E - (GROUPS - 1) * GE
            act.dma_start(grp_i[0:GROUPS - 1, :], dst[0:(GROUPS - 1) * GE].rearrange("(g e) -> g e", e=GE)).then_inc(indices_loaded, 16)
            act.dma_start(grp_i[GROUPS - 1:GROUPS, 0:rest], dst[(GROUPS - 1) * GE:E][None, :]).then_inc(indices_loaded, 16)
            act.dma_start(grp_i[GROUPS - 1:GROUPS, rest:GE], dst[E - (GE - rest):E][None, :]).then_inc(indices_loaded, 16)
            act.dma_start(dst_i[:], dst_t).then_inc(indices_loaded, 16)
            act.dma_start(src_idx[:], src_t).then_inc(indices_loaded, 16)
            act.dma_start(ident[:], ident_d).then_inc(consts_loaded, 16)
            act.dma_start(iota_row[:], iota_d[None, :].to_broadcast([P, WIN])).then_inc(consts_loaded, 16)
            act.dma_start(iota_part[:], iota_d[:, None]).then_inc(consts_loaded, 16)
            act.dma_start(bias_tab[:, 0:H], b1[None, :].to_broadcast([P, H])).then_inc(consts_loaded, 16)
            act.dma_start(bias_tab[:, H:], bg[None, :].to_broadcast([P, H])).then_inc(consts_loaded, 16)
            act.dma_start(gamma_b[:], gamma[None, :].to_broadcast([P, H])).then_inc(consts_loaded, 16)
            act.dma_start(beta_b[:], beta[None, :].to_broadcast([P, H])).then_inc(consts_loaded, 16)
            for k in range(2):
                for t in range(2):
                    act.dma_start(b2_raw[32 * k:32 * k + 1, t * H:(t + 1) * H], b2[None, :]).then_inc(consts_loaded, 16)
            act.dma_start(node_sum[0:N, :], x).then_inc(node_sum_set, 16)
            act.wait_ge(consts_set, 1)
            act.dma_start(node_sum[N:N + P, :], zero_rows[:]).then_inc(node_sum_set, 16)
            act.dma_start(node_sum[N + P:SUM_ROWS, :], zero_rows[0:SUM_ROWS - N - P, :]).then_inc(node_sum_set, 16)

            act.wait_ge(weights_loaded, 16 * W_LOADS)
            nc.scalar.activation(wtab_hi[:], wtab_raw[:], ACT.Copy).then_inc(w_hi_done, 1)

            for c in range(XCHUNKS):
                n = min(XN, N - c * XN)
                act.wait_ge(x_loaded[c % 2], 16 * (c // 2 + 1))
                if c >= 2:
                    act.wait_ge(table_mm, (c - 1) * XC)
                nc.scalar.activation(x_hi[:, c % 2, :, 0:n], x_raw[:, c % 2, :, 0:n], ACT.Copy).then_inc(x_hi_done, 1)
                if c == 0:
                    nc.scalar.activation(we_hi[:], we_raw[:], ACT.Copy).then_inc(w_hi_done, 1)
                    nc.scalar.activation(w2_hi[:], w2_raw[:], ACT.Copy).then_inc(w_hi_done, 1)

            def ea_high(gc, h):
                act.wait_ge(ea_loaded[h], 16 * (gc + 1))
                nc.scalar.activation(ea_st[0:DE, h, :], ea_raw[:, h, :], ACT.Copy).then_inc(ea_hi_done, 1)

            def msg_high(k, p):
                act.wait_ge(msg_done, k + 1)
                nc.scalar.activation(m_hi[:, p], msg[:, p], ACT.Copy).then_inc(mhi_done, 1)

            def copy_sum(gc, fresh=False):
                act.wait_ge(seg_done, gc * PPG + PPG)
                if not fresh:
                    act.wait_ge(sum_added, gc * 16)
                nc.scalar.activation(win_sum[:], ps_sum, ACT.Copy).then_inc(sum_copied, 1)

            def act_group(ps, g, first=False, last=False, second=False):
                gc = ps * GROUPS + g
                for j in range(PPG):
                    k, p = gc * PPG + j, j % 2
                    act.wait_ge(h_ready, k + 1)
                    if not first or j >= 2:
                        act.wait_ge(core_ready, k - 1)
                    nc.scalar.activation(h_hi[:, p], ps_h[p], ACT.Relu).then_inc(hhi_done, 1)
                    act.wait_ge(gadd_done, k + 1)
                    nc.scalar.activation(gate[:, p], gate[:, p], ACT.Sigmoid).then_inc(gate_done, 1)
                    if j == 0:
                        ea_high(gc, 1)
                    if j == 2 and not last:
                        ea_high(gc + 1, 0)
                    if j == 2 and not first:
                        copy_sum(gc - 1, second)
                    if not first or j >= 1:
                        if not first or j >= 3:
                            act.wait_ge(seg_done, k - 2)
                        msg_high(k - 1, (j - 1) % 2)

            more = passes(act)
            with act.Fori(0, more + 1) as ps:
                pass_start(act, ps)
                ea_high(ps * GROUPS, 0)
                act_group(ps, 0, first=True)
                act_group(ps, 1, second=True)
                with act.Fori(2, GROUPS - 1) as g:
                    act_group(ps, g)
                act_group(ps, GROUPS - 1, last=True)
                k = ps * PAIRS + PAIRS
                act.wait_ge(seg_done, k - 2)
                msg_high(k - 1, 1)
                copy_sum(ps * GROUPS + (GROUPS - 1))

            def norm_apply(c, norm):
                rows, R, _ = norm_rows(c)
                q, i = c % 2, norm_order.index((c, norm))
                act.wait_ge(n_mv_done, i + 1)
                nc.scalar.activation(n_sd[0:rows, q, norm, 0:R], n_mv[0:rows, q, norm, 0:R, 1], ACT.Sqrt,
                                     bias=eps_t[0:rows, :]).then_inc(n_sd_done, 1)
                act.wait_ge(n_nm_done, i + 1)
                for r in range(R):
                    last = nc.scalar.activation(n_sum[0:rows, q, r, :], n_sum[0:rows, q, r, :], ACT.Identity,
                                                scale=n_rs[0:rows, q, norm, r:r + 1], bias=n_nm[0:rows, q, norm, r:r + 1])
                last.then_inc(n_applied, 1)

            for c, norm in norm_order:
                norm_apply(c, norm)

        @block.tensor
        def _(pe):
            pe.wait_ge(consts_set, 2)
            pe.wait_ge(diag_ready, 1)
            nc.tensor.matmul(ps_misc[:, 0:2 * GROUPS], ones[0:GROUPS, :], grp_diag[:].rearrange("g a b -> g (a b)"),
                             start=True, stop=True).then_inc(stats_spread, 1)

            for t in range(NT):
                c, tt = t // XC, t % XC
                m = min(P, N - t * P)
                if t == 0:
                    pe.wait_ge(w_lo_done, 1)
                if tt == 0:
                    pe.wait_ge(x_lo_done, c + 1)
                if t >= 2:
                    pe.wait_ge(table_biased, t - 1)
                terms = [(a, b, k) for k in range(2) for a, b in ((x_hi, wtab_hi), (x_hi, wtab_lo), (x_lo, wtab_hi))]
                for i, (a, b, k) in enumerate(terms):
                    mm = nc.tensor.matmul(bank[t % 2][0:m, :], a[:, c % 2, k, tt * P:tt * P + m], b[:, k, :],
                                          start=(i == 0), stop=(i == len(terms) - 1))
                mm.then_inc(table_mm, 1)

            def front(k, gc, j, first):
                p, half = j % 2, j // 2
                if not first or j >= 2:
                    pe.wait_ge(hlo_done, k - 1)
                for t in range(2):
                    pe.wait_ge(gathered[2 * j + t], 16 * (gc + 1))
                    for c in range(2):
                        nc.tensor.matmul(ps_h[p][:, c, t * P:(t + 1) * P], gat[:, 2 * j + t, c * P:(c + 1) * P],
                                         ident[:], start=(t == 0 and c == 0), stop=False, is_transpose=True,
                                         skip_group_check=True)
                if j % 2 == 0:
                    pe.wait_ge(ea_lo_done, gc * 2 + (half + 1))
                ea = ea_st[:, half, (j % 2) * 2 * P:(j % 2 + 1) * 2 * P]
                for c in range(2):
                    for w in (we_hi, we_lo):
                        mm = nc.tensor.matmul(ps_h[p][:, c, :], w[:, c * P:(c + 1) * P], ea, start=False,
                                              stop=(c == 1 and w is we_lo), skip_group_check=True)
                mm.then_inc(h_ready, 1)
                if not first or j >= 2:
                    pe.wait_ge(gadd_done, k - 1)
                for t in range(2):
                    for w in (we_hi, we_lo):
                        mm = nc.tensor.matmul(ps_g[p][:, t, :], ea[:, t * P:(t + 1) * P], w[:, H:],
                                              start=(w is we_hi), stop=(w is we_lo))
                mm.then_inc(g_ready, 1)

            def core(k, j, early):
                p = j % 2
                if not early:
                    pe.wait_ge(msg_done, k - 1)
                nc.tensor.matmul(ps_c[p].rearrange("p t f -> p (t f)"), b2_sel[:], b2_parts[:], start=True,
                                 stop=False, skip_group_check=True)
                pe.wait_ge(hlo_done, k + 1)
                for t in range(2):
                    terms = [(a, b, c) for c in range(2) for a, b in ((h_hi, w2_hi), (h_hi, w2_lo), (h_lo, w2_hi))]
                    for i, (a, b, c) in enumerate(terms):
                        mm = nc.tensor.matmul(ps_c[p][:, t, :], a[:, p, c, t * P:(t + 1) * P], b[:, c, :],
                                              start=False, stop=(t == 1 and i == len(terms) - 1),
                                              skip_group_check=True)
                mm.then_inc(core_ready, 1)

            def segment(k, gc, j, first=False):
                p = j % 2
                if j == 0 and not first:
                    pe.wait_ge(sum_copied, gc)
                pe.wait_ge(sel_ready, k + 1)
                pe.wait_ge(mlo_done, k + 1)
                for t in range(2):
                    for m in (m_hi, m_lo):
                        mm = nc.tensor.matmul(ps_sum, sel[:, j, t, :], m[:, p, t, :],
                                              start=(j == 0 and t == 0 and m is m_hi),
                                              stop=(j == PPG - 1 and t == 1 and m is m_lo))
                mm.then_inc(seg_done, 1)

            def pe_group(ps, g, first=False):
                gc = ps * GROUPS + g
                for j in range(PPG):
                    k = gc * PPG + j
                    front(k, gc, j, first)
                    if not first or j >= 1:
                        core(k - 1, (j - 1) % PPG, first and j < 3)
                    if not first or j >= 2:
                        segment(k - 2, gc if j >= 2 else gc - 1, (j - 2) % PPG, first)

            pe.wait_ge(w_lo_done, 4)
            more = passes(pe)
            with pe.Fori(0, more + 1) as ps:
                pass_start(pe, ps)
                pe_group(ps, 0, first=True)
                with pe.Fori(1, GROUPS) as g:
                    pe_group(ps, g)
                gc = ps * GROUPS + (GROUPS - 1)
                k = gc * PPG + PPG
                core(k - 1, PPG - 1, False)
                segment(k - 2, gc, PPG - 2)
                segment(k - 1, gc, PPG - 1)

        @block.vector
        def _(dve):
            nc.vector.memset(zero_rows[:], 0.0).then_inc(consts_set, 1)
            nc.vector.memset(ones[:], 1.0).then_inc(consts_set, 1)
            nc.vector.memset(eps_t[:], EPS)
            nc.vector.memset(b2_parts[:].bitcast(F32), 0.0)
            nc.vector.memset(b2_sel[:].bitcast(F32), 0.0).then_inc(b2_step, 1)

            dve.wait_ge(indices_loaded, 16 * 5)
            dve.wait_ge(consts_loaded, 16 * C_LOADS)
            nc.vector.tensor_copy(dst_f[:], dst_i[:])
            nc.vector.tensor_copy(grp_f[:], grp_i[:]).then_inc(stat_step, 1)
            dve.wait_ge(stat_step, 1)
            nc.vector.tensor_reduce(grp_min[:], grp_f[:], AX_X, ALU.min)
            nc.vector.tensor_reduce(grp_max[:], grp_f[:], AX_X, ALU.max).then_inc(stat_step, 1)
            dve.wait_ge(stat_step, 2)
            nc.vector.tensor_tensor(grp_span[:], grp_max[:], grp_min[:], ALU.subtract).then_inc(stat_step, 1)
            dve.wait_ge(stat_step, 3)
            nc.vector.tensor_scalar(grp_diag[:, 0, :], ident[0:GROUPS, 0:GROUPS], grp_min[:, 0:1], None, ALU.mult)
            nc.vector.tensor_scalar(grp_diag[:, 1, :], ident[0:GROUPS, 0:GROUPS], grp_span[:, 0:1], None,
                                    ALU.mult).then_inc(diag_ready, 1)

            dve.wait_ge(w_hi_done, 1)
            nc.vector.tensor_tensor(wtab_lo[:], wtab_raw[:], wtab_hi[:].bitcast(F32), ALU.subtract).then_inc(w_lo_done, 1)

            def x_low(c):
                n = min(XN, N - c * XN)
                dve.wait_ge(x_hi_done, c + 1)
                nc.vector.tensor_tensor(x_lo[:, c % 2, :, 0:n], x_raw[:, c % 2, :, 0:n],
                                        x_hi[:, c % 2, :, 0:n].bitcast(F32), ALU.subtract).then_inc(x_lo_done, 1)

            x_low(0)
            dve.wait_ge(stats_spread, 1)
            nc.vector.tensor_copy(win_base[:], ps_misc[:, 0:GROUPS]).then_inc(windows_moved, 1)
            nc.vector.tensor_reduce(span_max[:], ps_misc[:, GROUPS:2 * GROUPS], AX_X, ALU.max).then_inc(stat_step, 1)
            dve.wait_ge(stat_step, 4)
            nc.vector.tensor_copy(span_int[:], span_max[:]).then_inc(stat_step, 1)
            dve.wait_ge(stat_step, 5)
            nc.vector.tensor_scalar(more_passes[:], span_int[:], WIN.bit_length() - 1, None,
                                    ALU.arith_shift_right).then_inc(passes_known, 1)
            dve.wait_ge(w_hi_done, 3)
            nc.vector.tensor_tensor(we_lo[:], we_raw[:], we_hi[:].bitcast(F32), ALU.subtract).then_inc(w_lo_done, 1)
            nc.vector.tensor_tensor(w2_lo[:], w2_raw[:], w2_hi[:].bitcast(F32), ALU.subtract).then_inc(w_lo_done, 1)
            dve.wait_ge(b2_step, 1)
            nc.vector.tensor_copy(b2_sel[0:1, :], ones[0:1, :])
            nc.vector.tensor_copy(b2_sel[32:33, :], ones[32:33, :])
            nc.vector.tensor_copy(b2_parts[0:1, :], b2_raw[0:1, :])
            nc.vector.tensor_copy(b2_hi[32:33, :], b2_raw[32:33, :]).then_inc(b2_step, 1)
            dve.wait_ge(b2_step, 2)
            nc.vector.tensor_tensor(b2_parts[32:33, :], b2_raw[32:33, :], b2_hi[32:33, :].bitcast(F32),
                                    ALU.subtract).then_inc(w_lo_done, 1)

            for t in range(NT):
                c, tt = t // XC, t % XC
                m = min(P, N - t * P)
                if tt == 0 and c == 0:
                    x_low(1)
                if tt == 1 and 1 <= c < XCHUNKS - 1:
                    x_low(c + 1)
                dve.wait_ge(table_mm, t + 1)
                if t >= 2:
                    dve.wait_ge(table_stored[t % 2], 16 * (t // 2))
                nc.vector.tensor_tensor(tab_out[0:m, t % 2, :], bank[t % 2][0:m, :], bias_tab[0:m, :],
                                        ALU.add).then_inc(table_biased, 1)

            def message(k, p):
                dve.wait_ge(core_ready, k + 1)
                dve.wait_ge(gate_done, k + 1)
                nc.vector.tensor_tensor(msg[:, p], ps_c[p], gate[:, p], ALU.mult).then_inc(msg_done, 1)

            def msg_low(k, p):
                dve.wait_ge(mhi_done, k + 1)
                nc.vector.tensor_tensor(m_lo[:, p], msg[:, p], m_hi[:, p].bitcast(F32), ALU.subtract).then_inc(mlo_done, 1)

            def dve_group(ps, g, first=False):
                gc = ps * GROUPS + g
                for j in range(PPG):
                    k, p = gc * PPG + j, j % 2
                    dve.wait_ge(g_ready, k + 1)
                    nc.vector.tensor_tensor(gate[:, p], ps_g[p], gat[:, 2 * j:2 * j + 2, H:], ALU.add).then_inc(gadd_done, 1)
                    dve.wait_ge(hhi_done, k + 1)
                    nc.vector.scalar_tensor_tensor(out=h_lo[:, p], in0=ps_h[p], scalar=0.0, in1=h_hi[:, p].bitcast(F32),
                                                   op0=ALU.max, op1=ALU.subtract).then_inc(hlo_done, 1)
                    if not first or j >= 1:
                        message(k - 1, (j - 1) % 2)
                    if not first:
                        dve.wait_ge(seg_done, k - 3)
                    rel = dst_rel[:, bass.ds(g * TPG + 2 * j, 2)]
                    nc.vector.tensor_tensor(sel[:, j], iota_row[:, None, :].to_broadcast([P, 2, WIN]),
                                            rel[:, :, None].to_broadcast([P, 2, WIN]), ALU.is_equal).then_inc(sel_ready, 1)
                    if not first or j >= 1:
                        msg_low(k - 1, (j - 1) % 2)

            more = passes(dve)
            with dve.Fori(0, more + 1) as ps:
                pass_start(dve, ps)
                dve.wait_ge(windows_moved, ps + 1)
                nc.vector.tensor_tensor(dst_rel[:].rearrange("p (g t) -> p g t", t=TPG),
                                        dst_f[:].rearrange("p (g t) -> p g t", t=TPG),
                                        win_base[:, :, None].to_broadcast([P, GROUPS, TPG]), ALU.subtract)
                nc.vector.tensor_scalar(sum_idx[:], win_base[:], float(N), iota_part[:, 0:1], ALU.min,
                                        ALU.add).then_inc(windows_set, 1)
                dve.wait_ge(windows_set, ps + 1)
                nc.vector.tensor_scalar(win_base[:], win_base[:], float(WIN), None, ALU.add).then_inc(windows_moved, 1)
                dve.wait_ge(windows_moved, ps + 2)
                dve_group(ps, 0, first=True)
                with dve.Fori(1, GROUPS) as g:
                    dve_group(ps, g)
                k = ps * PAIRS + PAIRS
                message(k - 1, 1)
                msg_low(k - 1, 1)

            def norm_stats(c, norm):
                rows, R, _ = norm_rows(c)
                q, i = c % 2, norm_order.index((c, norm))
                for r in range(R):
                    last = nc.vector.bn_stats(n_bn[0:rows, q, r, :], n_sum[0:rows, q, r, :])
                last.then_inc(n_bn_done, 1)
                dve.wait_ge(n_bn_done, i + 1)
                for r in range(R):
                    last = nc.vector.bn_aggr(n_mv[0:rows, q, norm, r, :], n_bn[0:rows, q, r, :])
                last.then_inc(n_mv_done, 1)

            def norm_scales(c, norm):
                rows, R, _ = norm_rows(c)
                q, i = c % 2, norm_order.index((c, norm))
                dve.wait_ge(n_sd_done, i + 1)
                nc.vector.reciprocal(n_rs[0:rows, q, norm, 0:R], n_sd[0:rows, q, norm, 0:R]).then_inc(n_rs_done, 1)
                dve.wait_ge(n_rs_done, i + 1)
                nc.vector.scalar_tensor_tensor(out=n_nm[0:rows, q, norm, 0:R], in0=n_mv[0:rows, q, norm, 0:R, 0],
                                               scalar=-1.0, in1=n_rs[0:rows, q, norm, 0:R], op0=ALU.mult,
                                               op1=ALU.mult).then_inc(n_nm_done, 1)

            def norm_middle(c):
                rows, R, _ = norm_rows(c)
                q, i = c % 2, norm_order.index((c, 0))
                v = n_sum[0:rows, q, 0:R, :]
                dve.wait_ge(n_applied, i + 1)
                nc.vector.tensor_tensor(v, v, gamma_b[0:rows, None, :].to_broadcast([rows, R, H]), ALU.mult).then_inc(n_scaled, 1)
                dve.wait_ge(n_scaled, c + 1)
                dve.wait_ge(n_xb_done, c + 1)
                nc.vector.tensor_tensor(v, v, n_x[0:rows, q, 0:R, :], ALU.add).then_inc(n_mid_done, 1)
                dve.wait_ge(n_mid_done, c + 1)

            for c, norm in norm_order:
                if norm == 0:
                    dve.wait_ge(n_loaded[c % 2], 32 * (c // 2 + 1))
                else:
                    norm_middle(c)
                norm_stats(c, norm)
                norm_scales(c, norm)

        @block.gpsimd
        def _(pool):
            def waited():
                pool.sem_inc(pool_waited, 1)

            def copy_gather_idx(gc, g, h):
                if g is not None:
                    count = gc * 16
                    for t in range(4 * h, 4 * h + 4):
                        pool.wait_ge(gathered[t], count)
                waited()
                cols = bass.ds((0 if g is None else g) * TPG + 4 * h, 4)
                nc.gpsimd.tensor_copy(gat_idx[:, 4 * h:4 * h + 4], src_idx[:, cols]).then_inc(idx_copied, 1)
                count = gc * 2 + (h + 1)
                pool.wait_ge(idx_copied, count)
                waited()

            def gather(k, j, first):
                if not first:
                    count = k - 3
                    pool.wait_ge(h_ready, count)
                    pool.wait_ge(gadd_done, count)
                    waited()
                for t in range(2 * j, 2 * j + 2):
                    nc.gpsimd.indirect_dma_start(
                        gat[:, t, :], None, node_table,
                        bass.IndirectOffsetOnAxis(ap=gat_idx[:, t:t + 1], axis=0)).then_inc(gathered[t], 16)

            def ea_low(gc, h):
                pool.wait_ge(ea_hi_done, gc * 2 + (h + 1))
                nc.gpsimd.tensor_tensor(ea_st[DE:2 * DE, h, :], ea_raw[:, h, :], ea_st[0:DE, h, :].bitcast(F32),
                                        ALU.subtract).then_inc(ea_lo_done, 1)
                pool.wait_ge(ea_lo_done, gc * 2 + (h + 1))
                waited()

            def add_sum(gc, g, fresh=False):
                if not fresh:
                    pool.wait_ge(sum_added, gc * 16)
                    waited()
                nc.gpsimd.tensor_copy(sct_idx[:], sum_idx[:, bass.ds(g, 1)]).then_inc(sct_idx_copied, 1)
                count = gc + 1
                pool.wait_ge(sct_idx_copied, count)
                pool.wait_ge(sum_copied, count)
                waited()
                nc.gpsimd.indirect_dma_start(
                    node_sum, bass.IndirectOffsetOnAxis(ap=sct_idx[:, 0:1], axis=0), win_sum[:], None,
                    compute_op=ALU.add).then_inc(sum_added, 16)

            def pool_group(ps, g, first=False, sums=True, fresh=False):
                gc = ps * GROUPS + g
                if not first:
                    ea_low(gc - 1, 1)
                copy_gather_idx(gc, None if first else g, 0)
                gather(gc * PPG, 0, first)
                gather(gc * PPG + 1, 1, first)
                if sums:
                    add_sum(gc - 2, g - 2, fresh)
                ea_low(gc, 0)
                copy_gather_idx(gc, None if first else g, 1)
                gather(gc * PPG + 2, 2, first)
                gather(gc * PPG + 3, 3, first)

            pool.wait_ge(indices_loaded, 16 * 5)
            pool.wait_ge(node_sum_set, 16 * 3)
            for i in range(2):
                pool.wait_ge(table_stored[i], 16 * ((NT + 1 - i) // 2))
            pool.sem_inc(pass_open, 1)
            more = passes(pool)
            with pool.Fori(0, more + 1) as ps:
                pass_start(pool, ps)
                pool.wait_ge(windows_set, ps + 1)
                pool_group(ps, 0, first=True, sums=False)
                pool_group(ps, 1, sums=False)
                pool_group(ps, 2, fresh=True)
                with pool.Fori(3, GROUPS) as g:
                    pool_group(ps, g)
                last = ps * GROUPS + (GROUPS - 1)
                ea_low(last, 1)
                add_sum(last - 1, GROUPS - 2)
                add_sum(last, GROUPS - 1)
                pool.wait_ge(sum_added, last * 16 + 16)
                pool.sem_inc(pass_open, 1)

            for c in range(NCHUNKS + 1):
                rows, R, _ = norm_rows(c)
                v = n_x[0:rows, c % 2, 0:R, :]
                pool.wait_ge(n_loaded[c % 2], 32 * (c // 2 + 1))
                nc.gpsimd.tensor_tensor(v, v, beta_b[0:rows, None, :].to_broadcast([rows, R, H]), ALU.add).then_inc(n_xb_done, 1)


def kernel(x, src, dst, edge_attr_64, L0_gnn_W1, L0_gnn_b1, L0_gnn_W2, L0_gnn_b2, L0_gnn_Wg, L0_gnn_bg,
           L0_gnn_gamma, L0_gnn_beta):
    import numpy as np
    import concourse.bacc as bacc
    from concourse import mybir as mb
    from concourse.bass_utils import run_bass_kernel_spmd

    x, src, dst, ea = (np.asarray(a) for a in (x, src, dst, edge_attr_64))
    pad = TILES * P - E
    arrays = {
        "xT": np.ascontiguousarray(x.T),
        "x": np.ascontiguousarray(x),
        "src_t": np.ascontiguousarray(np.pad(src, (0, pad)).reshape(TILES, P).T),
        "dst_t": np.ascontiguousarray(np.pad(dst, (0, pad), constant_values=-1).reshape(TILES, P).T),
        "dst": np.ascontiguousarray(dst),
        "eaT": np.ascontiguousarray(np.pad(ea, ((0, pad), (0, 0))).reshape(GROUPS, GE, DE).transpose(0, 2, 1)),
        "w1": np.ascontiguousarray(L0_gnn_W1), "b1": np.ascontiguousarray(L0_gnn_b1),
        "w2": np.ascontiguousarray(L0_gnn_W2), "b2": np.ascontiguousarray(L0_gnn_b2),
        "wg": np.ascontiguousarray(L0_gnn_Wg), "bg": np.ascontiguousarray(L0_gnn_bg),
        "gamma": np.ascontiguousarray(L0_gnn_gamma), "beta": np.ascontiguousarray(L0_gnn_beta),
        "ident_d": np.eye(P, dtype=np.float32),
        "iota_d": np.arange(P, dtype=np.float32),
    }
    nc = bacc.Bacc("TRN2", target_bir_lowering=False, num_devices=1)
    args = [nc.dram_tensor("in_" + k, a.shape, mb.dt.from_np(a.dtype), kind="ExternalInput").ap()
            for k, a in arrays.items()]
    out = nc.dram_tensor("out", (N, H), mb.dt.float32, kind="ExternalOutput").ap()
    gnn_program(nc, *args, out)
    r = run_bass_kernel_spmd(nc, [{"in_" + k: a for k, a in arrays.items()}], core_ids=[0])
    return r.results[0]["out"]
```

```python
from contextlib import ExitStack

import concourse.bass as bass
from concourse import mybir

F32 = mybir.dt.float32
F32R = mybir.dt.float32r
I32 = mybir.dt.int32
ALU = mybir.AluOpType
ACT = mybir.ActivationFunctionType
AX_X = mybir.AxisListType.X

P = 128
N, H, DE, E = 6250, 256, 64, 106250
EPS = 1e-5
TPG = 8
PPG = TPG // 2
GROUPS = -(-E // (TPG * P))
TILES = GROUPS * TPG
PAIRS = GROUPS * PPG
GE = TPG * P
HALF = GE // 2
WIN = P
SUM_ROWS = -(-(N + WIN) // P) * P
NT = -(-N // P)
XC = 7
XCHUNKS = NT // XC
XN = XC * P
NR = 8
NCHUNKS = N // (P * NR)
NREST = N - NCHUNKS * P * NR


def gnn_program(nc, xT, x, src_t, dst_t, dst, eaT, w1, b1, w2, b2, wg, bg, gamma, beta, ident_d, iota_d, out):
    assert NT == XC * XCHUNKS and 0 < NREST <= P
    node_table = nc.dram_tensor("node_table", (N, 2 * H), F32).ap()
    node_sum = nc.dram_tensor("node_sum", (SUM_ROWS, H), F32).ap()
    with ExitStack() as ctx:
        def sb(name, shape, dt=F32):
            return ctx.enter_context(nc.sbuf_tensor(name, shape, dt))

        def sem(name):
            return ctx.enter_context(nc.semaphore(name))

        bank = [ctx.enter_context(nc.psum_tensor(f"bank{i}", [P, 512], F32)) for i in range(8)]
        ps_h = [bank[i][:, :].rearrange("p (c e) -> p c e", c=2) for i in (0, 1)]
        ps_g = [bank[i][:, :].rearrange("p (t f) -> p t f", t=2) for i in (2, 3)]
        ps_c = [bank[i][:, :].rearrange("p (t f) -> p t f", t=2) for i in (4, 5)]
        ps_sum = bank[6][:, 0:H]
        ps_misc = bank[7]

        ident = sb("ident", [P, P])
        ident_r = sb("ident_r", [P, P], F32R)
        iota_row = sb("iota_row", [P, WIN])
        iota_part = sb("iota_part", [P, 1])
        ones = sb("ones", [P, P])
        wtab_raw = sb("wtab_raw", [P, 2, 2 * H])
        wtab_hi = sb("wtab_hi", [P, 2, 2 * H], F32R)
        wtab_lo = sb("wtab_lo", [P, 2, 2 * H], F32R)
        we_raw = sb("we_raw", [P, 2 * H])
        we_hi = sb("we_hi", [P, 2 * H], F32R)
        we_lo = sb("we_lo", [P, 2 * H], F32R)
        w2_raw = sb("w2_raw", [P, 2, H])
        w2_hi = sb("w2_hi", [P, 2, H], F32R)
        w2_lo = sb("w2_lo", [P, 2, H], F32R)
        b2_b = sb("b2_b", [P, 2, H])
        bias_tab = sb("bias_tab", [P, 2 * H])
        gamma_b = sb("gamma_b", [P, H])
        beta_b = sb("beta_b", [P, H])
        eps_t = sb("eps_t", [P, 1])

        src_idx = sb("src_idx", [P, TILES], I32)
        dst_i = sb("dst_i", [P, TILES], I32)
        dst_f = sb("dst_f", [P, TILES])
        dst_rel = sb("dst_rel", [P, TILES])
        grp_i = sb("grp_i", [GROUPS, GE], I32)
        grp_f = sb("grp_f", [GROUPS, GE])
        grp_min = sb("grp_min", [GROUPS, 1])
        grp_max = sb("grp_max", [GROUPS, 1])
        grp_span = sb("grp_span", [GROUPS, 1])
        grp_diag = sb("grp_diag", [GROUPS, 2, GROUPS])
        win_base = sb("win_base", [P, GROUPS])
        win_clip = sb("win_clip", [P, GROUPS])
        sum_idx = sb("sum_idx", [P, GROUPS], I32)
        span_max = sb("span_max", [P, 1])
        span_int = sb("span_int", [P, 1], I32)
        more_passes = sb("more_passes", [P, 1], I32)

        gat = sb("gat", [P, TPG, 2 * H])
        gat_idx = sb("gat_idx", [P, TPG], I32)
        sct_idx = sb("sct_idx", [P, 1], I32)
        ea_raw = sb("ea_raw", [DE, 2, HALF])
        ea_st = sb("ea_st", [P, PPG, 2 * P], F32R)
        h_hi = sb("h_hi", [P, 2, 2, 2 * P], F32R)
        h_lo = sb("h_lo", [P, 2, 2, 2 * P], F32R)
        gate = sb("gate", [P, 2, 2, H])
        msg = sb("msg", [P, 2, 2, H])
        m_hi = sb("m_hi", [P, 2, 2, H], F32R)
        m_lo = sb("m_lo", [P, 2, 2, H], F32R)
        sel = sb("sel", [P, PPG, 2, WIN], F32R)
        win_sum = sb("win_sum", [P, H])

        x_raw = sb("x_raw", [P, 2, 2, XN])
        x_hi = sb("x_hi", [P, 2, 2, XN], F32R)
        x_lo = sb("x_lo", [P, 2, 2, XN], F32R)
        tab_out = sb("tab_out", [P, 2, 2 * H])
        zero_rows = sb("zero_rows", [P, H])

        n_sum = sb("n_sum", [P, 2, NR, H])
        n_x = sb("n_x", [P, 2, NR, H])
        n_bn = sb("n_bn", [P, 2, NR, 6])
        n_mv = sb("n_mv", [P, 2, 2, NR, 2])
        n_sd = sb("n_sd", [P, 2, 2, NR])
        n_rs = sb("n_rs", [P, 2, 2, NR])
        n_nm = sb("n_nm", [P, 2, 2, NR])

        consts_set = sem("consts_set")
        consts_loaded = sem("consts_loaded")
        weights_loaded = sem("weights_loaded")
        indices_loaded = sem("indices_loaded")
        w_hi_done = sem("w_hi_done")
        w_lo_done = sem("w_lo_done")
        banks_primed = sem("banks_primed")
        stat_step = sem("stat_step")
        diag_ready = sem("diag_ready")
        stats_spread = sem("stats_spread")
        passes_known = sem("passes_known")
        windows_set = sem("windows_set")
        windows_moved = sem("windows_moved")
        x_loaded = [sem(f"x_loaded{i}") for i in range(2)]
        x_hi_done = sem("x_hi_done")
        x_lo_done = sem("x_lo_done")
        table_mm = sem("table_mm")
        table_biased = sem("table_biased")
        table_stored = [sem(f"table_stored{i}") for i in range(2)]
        node_sum_set = sem("node_sum_set")
        ea_loaded = [sem(f"ea_loaded{i}") for i in range(2)]
        ea_hi_done = sem("ea_hi_done")
        ea_lo_done = sem("ea_lo_done")
        idx_copied = sem("idx_copied")
        gathered = [sem(f"gathered{i}") for i in range(TPG)]
        h_ready = sem("h_ready")
        g_ready = sem("g_ready")
        hhi_done = sem("hhi_done")
        hlo_done = sem("hlo_done")
        g_seeded = sem("g_seeded")
        c_seeded = sem("c_seeded")
        gate_done = sem("gate_done")
        core_ready = sem("core_ready")
        msg_done = sem("msg_done")
        mhi_done = sem("mhi_done")
        mlo_done = sem("mlo_done")
        sel_ready = sem("sel_ready")
        seg_done = sem("seg_done")
        sum_copied = sem("sum_copied")
        pool_waited = sem("pool_waited")
        sum_added = sem("sum_added")
        pass_open = sem("pass_open")
        sct_idx_copied = sem("sct_idx_copied")
        n_loaded = [sem(f"n_loaded{i}") for i in range(2)]
        n_bn_done = sem("n_bn_done")
        n_mv_done = sem("n_mv_done")
        n_sd_done = sem("n_sd_done")
        n_rs_done = sem("n_rs_done")
        n_nm_done = sem("n_nm_done")
        n_applied = sem("n_applied")
        n_xb_done = sem("n_xb_done")
        n_scaled = sem("n_scaled")
        n_mid_done = sem("n_mid_done")
        n_stored = [sem(f"n_stored{i}") for i in range(2)]

        xT_v = xT.rearrange("(c p) n -> p c n", c=2)
        W_LOADS = 9
        C_LOADS = 9
        norm_order = [(0, 0)]
        for c in range(NCHUNKS + 1):
            norm_order += [(c + 1, 0)] * (c < NCHUNKS) + [(c, 1)]

        block = ctx.enter_context(nc.Block())

        def passes(eng):
            eng.wait_ge(passes_known, 1)
            return eng.value_load(more_passes[0:1, 0:1], min_val=0, max_val=N // WIN + 1)

        def pass_start(eng, ps):
            eng.wait_ge(pass_open, ps + 1)

        def norm_rows(c):
            first = c * P * NR
            if c < NCHUNKS:
                return P, NR, slice(first, first + P * NR)
            return NREST, 1, slice(first, N)

        @block.sync
        def _(sp):
            sp.dma_start(x_raw[:, 0], xT_v[:, :, 0:XN]).then_inc(x_loaded[0], 16)
            for c in range(2):
                sp.dma_start(wtab_raw[:, c, 0:H], w1[c * P:(c + 1) * P, :]).then_inc(weights_loaded, 16)
                sp.dma_start(wtab_raw[:, c, H:], wg[c * P:(c + 1) * P, :]).then_inc(weights_loaded, 16)
            for k in range(2):
                sp.dma_start(we_raw[k * DE:(k + 1) * DE, 0:H], w1[H:H + DE, :]).then_inc(weights_loaded, 16)
                sp.dma_start(we_raw[k * DE:(k + 1) * DE, H:], wg[H:H + DE, :]).then_inc(weights_loaded, 16)
            sp.dma_start(w2_raw[:], w2.rearrange("(c p) f -> p c f", c=2)).then_inc(weights_loaded, 16)
            sp.dma_start(x_raw[:, 1], xT_v[:, :, XN:2 * XN]).then_inc(x_loaded[1], 16)

            for t in range(NT):
                c, tt = t // XC, t % XC
                if tt == 0 and 1 <= c and c + 1 < XCHUNKS:
                    n = min(XN, N - (c + 1) * XN)
                    sp.wait_ge(x_lo_done, c)
                    sp.dma_start(x_raw[:, (c + 1) % 2, :, 0:n],
                                 xT_v[:, :, (c + 1) * XN:(c + 1) * XN + n]).then_inc(x_loaded[(c + 1) % 2], 16)
                m = min(P, N - t * P)
                sp.wait_ge(table_biased, t + 1)
                sp.dma_start(node_table[t * P:t * P + m, :], tab_out[0:m, t % 2, :]).then_inc(table_stored[t % 2], 16)

            more = passes(sp)
            with sp.Fori(0, more + 1) as ps:
                pass_start(sp, ps)
                for h in range(2):
                    sp.dma_start(ea_raw[:, h, :], eaT[0, :, h * HALF:(h + 1) * HALF]).then_inc(ea_loaded[h], 16)
                with sp.Fori(1, GROUPS) as g:
                    for h in range(2):
                        sp.wait_ge(ea_lo_done, (ps * GROUPS + g) * PPG + (2 * h + 2 - PPG))
                        sp.dma_start(ea_raw[:, h, :], eaT[bass.ds(g, 1), :, h * HALF:(h + 1) * HALF].rearrange(
                            "o d e -> (o d) e")).then_inc(ea_loaded[h], 16)

            sp.wait_ge(pass_open, more + 2)
            for c in range(NCHUNKS + 1 + 2):
                if c >= 2:
                    q, (rows, R, at) = (c - 2) % 2, norm_rows(c - 2)
                    sp.wait_ge(n_applied, norm_order.index((c - 2, 1)) + 1)
                    sp.dma_start(out[at, :].rearrange("(p r) f -> p r f", r=R), n_sum[0:rows, q, 0:R, :]).then_inc(n_stored[q], 16)
                if c <= NCHUNKS:
                    q, (rows, R, at) = c % 2, norm_rows(c)
                    if c >= 2:
                        sp.wait_ge(n_stored[q], 16 * (c // 2))
                    sp.dma_start(n_sum[0:rows, q, 0:R, :], node_sum[at, :].rearrange("(p r) f -> p r f", r=R)).then_inc(n_loaded[q], 16)
                    sp.dma_start(n_x[0:rows, q, 0:R, :], x[at, :].rearrange("(p r) f -> p r f", r=R)).then_inc(n_loaded[q], 16)
            for q in range(2):
                sp.wait_ge(n_stored[q], 16 * ((NCHUNKS + 1 + 1 - q) // 2))

        @block.scalar
        def _(act):
            rest = E - (GROUPS - 1) * GE
            act.dma_start(grp_i[0:GROUPS - 1, :], dst[0:(GROUPS - 1) * GE].rearrange("(g e) -> g e", e=GE)).then_inc(indices_loaded, 16)
            act.dma_start(grp_i[GROUPS - 1:GROUPS, 0:rest], dst[(GROUPS - 1) * GE:E][None, :]).then_inc(indices_loaded, 16)
            act.dma_start(grp_i[GROUPS - 1:GROUPS, rest:GE], dst[E - (GE - rest):E][None, :]).then_inc(indices_loaded, 16)
            act.dma_start(dst_i[:], dst_t).then_inc(indices_loaded, 16)
            act.dma_start(src_idx[:], src_t).then_inc(indices_loaded, 16)
            act.dma_start(ident[:], ident_d).then_inc(consts_loaded, 16)
            act.dma_start(iota_row[:], iota_d[None, :].to_broadcast([P, WIN])).then_inc(consts_loaded, 16)
            act.dma_start(iota_part[:], iota_d[:, None]).then_inc(consts_loaded, 16)
            act.dma_start(bias_tab[:, 0:H], b1[None, :].to_broadcast([P, H])).then_inc(consts_loaded, 16)
            act.dma_start(bias_tab[:, H:], bg[None, :].to_broadcast([P, H])).then_inc(consts_loaded, 16)
            act.dma_start(gamma_b[:], gamma[None, :].to_broadcast([P, H])).then_inc(consts_loaded, 16)
            act.dma_start(beta_b[:], beta[None, :].to_broadcast([P, H])).then_inc(consts_loaded, 16)
            for t in range(2):
                act.dma_start(b2_b[:, t, :], b2[None, :].to_broadcast([P, H])).then_inc(consts_loaded, 16)
            act.dma_start(node_sum[0:N, :], x).then_inc(node_sum_set, 16)
            act.wait_ge(consts_set, 1)
            act.dma_start(node_sum[N:N + P, :], zero_rows[:]).then_inc(node_sum_set, 16)
            act.dma_start(node_sum[N + P:SUM_ROWS, :], zero_rows[0:SUM_ROWS - N - P, :]).then_inc(node_sum_set, 16)

            act.wait_ge(weights_loaded, 16 * W_LOADS)
            nc.scalar.activation(wtab_hi[:], wtab_raw[:], ACT.Copy).then_inc(w_hi_done, 1)

            for c in range(XCHUNKS):
                n = min(XN, N - c * XN)
                act.wait_ge(x_loaded[c % 2], 16 * (c // 2 + 1))
                if c >= 2:
                    act.wait_ge(table_mm, (c - 1) * XC)
                nc.scalar.activation(x_hi[:, c % 2, :, 0:n], x_raw[:, c % 2, :, 0:n], ACT.Copy).then_inc(x_hi_done, 1)
                if c == 0:
                    nc.scalar.activation(we_hi[:], we_raw[:], ACT.Copy).then_inc(w_hi_done, 1)
                    nc.scalar.activation(w2_hi[:], w2_raw[:], ACT.Copy).then_inc(w_hi_done, 1)

            def seed_gate(gc, j):
                for t in (2 * j, 2 * j + 1):
                    act.wait_ge(gathered[t], 16 * (gc + 1))
                nc.scalar.activation(ps_g[j % 2], gat[:, 2 * j:2 * j + 2, H:], ACT.Copy).then_inc(g_seeded, 1)

            def seed_core(j):
                nc.scalar.activation(ps_c[j % 2], b2_b[:], ACT.Copy).then_inc(c_seeded, 1)

            def msg_high(k, p):
                act.wait_ge(msg_done, k + 1)
                nc.scalar.activation(m_hi[:, p], msg[:, p], ACT.Copy).then_inc(mhi_done, 1)

            def copy_sum(gc, fresh=False):
                act.wait_ge(seg_done, gc * PPG + PPG)
                if not fresh:
                    act.wait_ge(sum_added, gc * 16)
                nc.scalar.activation(win_sum[:], ps_sum, ACT.Copy).then_inc(sum_copied, 1)

            def act_group(ps, g, first=False, last=False, second=False):
                gc = ps * GROUPS + g
                for j in range(PPG):
                    k, p = gc * PPG + j, j % 2
                    if j == PPG - 1 and not first:
                        copy_sum(gc - 1, second)
                    act.wait_ge(h_ready, k + 1)
                    if not first or j >= 2:
                        act.wait_ge(core_ready, k - 1)
                    nc.scalar.activation(h_hi[:, p], ps_h[p], ACT.Relu).then_inc(hhi_done, 1)
                    if not first or j >= 2:
                        if not first:
                            act.wait_ge(seg_done, k - 3)
                        msg_high(k - 2, p)
                    act.wait_ge(g_ready, k + 1)
                    if not first or j >= 2:
                        act.wait_ge(msg_done, k - 1)
                    nc.scalar.activation(gate[:, p], ps_g[p], ACT.Sigmoid).then_inc(gate_done, 1)
                    if not last or j < PPG - 1:
                        if not first or j >= 1:
                            act.wait_ge(gate_done, k)
                        seed_gate(gc + (j + 1) // PPG, (j + 1) % PPG)
                    seed_core(j)

            act.wait_ge(banks_primed, 1)
            more = passes(act)
            with act.Fori(0, more + 1) as ps:
                pass_start(act, ps)
                seed_gate(ps * GROUPS, 0)
                act_group(ps, 0, first=True)
                act_group(ps, 1, second=True)
                with act.Fori(2, GROUPS - 1) as g:
                    act_group(ps, g)
                act_group(ps, GROUPS - 1, last=True)
                k = ps * PAIRS + PAIRS
                for p in range(2):
                    act.wait_ge(seg_done, k - 3 + p)
                    msg_high(k - 2 + p, p)
                copy_sum(ps * GROUPS + (GROUPS - 1))

            def norm_apply(c, norm):
                rows, R, _ = norm_rows(c)
                q, i = c % 2, norm_order.index((c, norm))
                act.wait_ge(n_mv_done, i + 1)
                nc.scalar.activation(n_sd[0:rows, q, norm, 0:R], n_mv[0:rows, q, norm, 0:R, 1], ACT.Sqrt,
                                     bias=eps_t[0:rows, :]).then_inc(n_sd_done, 1)
                act.wait_ge(n_nm_done, i + 1)
                for r in range(R):
                    last = nc.scalar.activation(n_sum[0:rows, q, r, :], n_sum[0:rows, q, r, :], ACT.Identity,
                                                scale=n_rs[0:rows, q, norm, r:r + 1], bias=n_nm[0:rows, q, norm, r:r + 1])
                last.then_inc(n_applied, 1)

            for c, norm in norm_order:
                norm_apply(c, norm)

        @block.tensor
        def _(pe):
            pe.wait_ge(consts_set, 2)
            pe.wait_ge(diag_ready, 1)
            nc.tensor.matmul(ps_misc[:, 0:2 * GROUPS], ones[0:GROUPS, :], grp_diag[:].rearrange("g a b -> g (a b)"),
                             start=True, stop=True).then_inc(stats_spread, 1)

            pe.wait_ge(w_lo_done, 1)
            for i in (2, 3, 4, 5):
                mm = nc.tensor.matmul(bank[i][:, :], wtab_hi[:, 0, 0:P], wtab_hi[:, 1, :], start=True, stop=True)
            mm.then_inc(banks_primed, 1)

            for t in range(NT):
                c, tt = t // XC, t % XC
                m = min(P, N - t * P)
                if tt == 0:
                    pe.wait_ge(x_lo_done, c + 1)
                if t >= 2:
                    pe.wait_ge(table_biased, t - 1)
                terms = [(a, b, k) for k in range(2) for a, b in ((x_hi, wtab_hi), (x_hi, wtab_lo), (x_lo, wtab_hi))]
                for i, (a, b, k) in enumerate(terms):
                    mm = nc.tensor.matmul(bank[t % 2][0:m, :], a[:, c % 2, k, tt * P:tt * P + m], b[:, k, :],
                                          start=(i == 0), stop=(i == len(terms) - 1))
                mm.then_inc(table_mm, 1)

            def front(k, gc, j, first):
                p = j % 2
                if not first or j >= 2:
                    pe.wait_ge(hlo_done, k - 1)
                for t in range(2):
                    pe.wait_ge(gathered[2 * j + t], 16 * (gc + 1))
                    for c in range(2):
                        nc.tensor.matmul(ps_h[p][:, c, t * P:(t + 1) * P].bitcast(F32R),
                                         gat[:, 2 * j + t, c * P:(c + 1) * P].bitcast(F32R), ident_r[:],
                                         start=(t == 0 and c == 0), stop=False, is_transpose=True,
                                         skip_group_check=True)
                pe.wait_ge(ea_lo_done, k + 1)
                ea = ea_st[:, j, :]
                for c in range(2):
                    for w in (we_hi, we_lo):
                        mm = nc.tensor.matmul(ps_h[p][:, c, :], w[:, c * P:(c + 1) * P], ea, start=False,
                                              stop=(c == 1 and w is we_lo), skip_group_check=True)
                mm.then_inc(h_ready, 1)
                pe.wait_ge(g_seeded, k + 1)
                for t in range(2):
                    for w in (we_hi, we_lo):
                        mm = nc.tensor.matmul(ps_g[p][:, t, :], ea[:, t * P:(t + 1) * P], w[:, H:],
                                              start=False, stop=(w is we_lo), skip_group_check=True)
                mm.then_inc(g_ready, 1)

            def core(k, j):
                p = j % 2
                pe.wait_ge(c_seeded, k + 1)
                pe.wait_ge(hlo_done, k + 1)
                for t in range(2):
                    terms = [(a, b, c) for c in range(2) for a, b in ((h_hi, w2_hi), (h_hi, w2_lo), (h_lo, w2_hi))]
                    for i, (a, b, c) in enumerate(terms):
                        mm = nc.tensor.matmul(ps_c[p][:, t, :], a[:, p, c, t * P:(t + 1) * P], b[:, c, :],
                                              start=False, stop=(t == 1 and i == len(terms) - 1),
                                              skip_group_check=True)
                mm.then_inc(core_ready, 1)

            def segment(k, gc, j, first=False):
                p = j % 2
                if j == 0 and not first:
                    pe.wait_ge(sum_copied, gc)
                pe.wait_ge(sel_ready, k + 1)
                pe.wait_ge(mlo_done, k + 1)
                for t in range(2):
                    for m in (m_hi, m_lo):
                        mm = nc.tensor.matmul(ps_sum, sel[:, j, t, :], m[:, p, t, :],
                                              start=(j == 0 and t == 0 and m is m_hi),
                                              stop=(j == PPG - 1 and t == 1 and m is m_lo))
                mm.then_inc(seg_done, 1)

            def pe_group(ps, g, first=False):
                gc = ps * GROUPS + g
                for j in range(PPG):
                    k = gc * PPG + j
                    front(k, gc, j, first)
                    if not first or j >= 1:
                        core(k - 1, (j - 1) % PPG)
                    if not first or j >= 3:
                        segment(k - 3, gc if j >= 3 else gc - 1, (j - 3) % PPG, first)

            pe.wait_ge(w_lo_done, 3)
            more = passes(pe)
            with pe.Fori(0, more + 1) as ps:
                pass_start(pe, ps)
                pe_group(ps, 0, first=True)
                with pe.Fori(1, GROUPS) as g:
                    pe_group(ps, g)
                gc = ps * GROUPS + (GROUPS - 1)
                k = gc * PPG + PPG
                core(k - 1, PPG - 1)
                for j in range(1, PPG):
                    segment(gc * PPG + j, gc, j)

        @block.vector
        def _(dve):
            nc.vector.memset(zero_rows[:], 0.0).then_inc(consts_set, 1)
            nc.vector.memset(ones[:], 1.0).then_inc(consts_set, 1)
            nc.vector.memset(eps_t[:], EPS)

            dve.wait_ge(indices_loaded, 16 * 5)
            dve.wait_ge(consts_loaded, 16 * C_LOADS)
            nc.vector.tensor_copy(ident_r[:], ident[:])
            nc.vector.tensor_copy(dst_f[:], dst_i[:])
            nc.vector.tensor_copy(grp_f[:], grp_i[:]).then_inc(stat_step, 1)
            dve.wait_ge(stat_step, 1)
            nc.vector.tensor_reduce(grp_min[:], grp_f[:], AX_X, ALU.min)
            nc.vector.tensor_reduce(grp_max[:], grp_f[:], AX_X, ALU.max).then_inc(stat_step, 1)
            dve.wait_ge(stat_step, 2)
            nc.vector.tensor_tensor(grp_span[:], grp_max[:], grp_min[:], ALU.subtract).then_inc(stat_step, 1)
            dve.wait_ge(stat_step, 3)
            nc.vector.tensor_scalar(grp_diag[:, 0, :], ident[0:GROUPS, 0:GROUPS], grp_min[:, 0:1], None, ALU.mult)
            nc.vector.tensor_scalar(grp_diag[:, 1, :], ident[0:GROUPS, 0:GROUPS], grp_span[:, 0:1], None,
                                    ALU.mult).then_inc(diag_ready, 1)

            dve.wait_ge(w_hi_done, 1)
            nc.vector.tensor_tensor(wtab_lo[:], wtab_raw[:], wtab_hi[:].bitcast(F32), ALU.subtract).then_inc(w_lo_done, 1)

            def x_low(c):
                n = min(XN, N - c * XN)
                dve.wait_ge(x_hi_done, c + 1)
                nc.vector.tensor_tensor(x_lo[:, c % 2, :, 0:n], x_raw[:, c % 2, :, 0:n],
                                        x_hi[:, c % 2, :, 0:n].bitcast(F32), ALU.subtract).then_inc(x_lo_done, 1)

            x_low(0)
            dve.wait_ge(stats_spread, 1)
            nc.vector.tensor_copy(win_base[:], ps_misc[:, 0:GROUPS]).then_inc(windows_moved, 1)
            nc.vector.tensor_reduce(span_max[:], ps_misc[:, GROUPS:2 * GROUPS], AX_X, ALU.max).then_inc(stat_step, 1)
            dve.wait_ge(stat_step, 4)
            nc.vector.tensor_copy(span_int[:], span_max[:]).then_inc(stat_step, 1)
            dve.wait_ge(stat_step, 5)
            nc.vector.tensor_scalar(more_passes[:], span_int[:], WIN.bit_length() - 1, None,
                                    ALU.arith_shift_right).then_inc(passes_known, 1)
            dve.wait_ge(w_hi_done, 3)
            nc.vector.tensor_tensor(we_lo[:], we_raw[:], we_hi[:].bitcast(F32), ALU.subtract).then_inc(w_lo_done, 1)
            nc.vector.tensor_tensor(w2_lo[:], w2_raw[:], w2_hi[:].bitcast(F32), ALU.subtract).then_inc(w_lo_done, 1)
            for t in range(NT):
                c, tt = t // XC, t % XC
                m = min(P, N - t * P)
                if tt == 0 and c == 0:
                    x_low(1)
                if tt == 1 and 1 <= c < XCHUNKS - 1:
                    x_low(c + 1)
                dve.wait_ge(table_mm, t + 1)
                if t >= 2:
                    dve.wait_ge(table_stored[t % 2], 16 * (t // 2))
                nc.vector.tensor_tensor(tab_out[0:m, t % 2, :], bank[t % 2][0:m, :], bias_tab[0:m, :],
                                        ALU.add).then_inc(table_biased, 1)

            def message(k, p):
                dve.wait_ge(core_ready, k + 1)
                dve.wait_ge(gate_done, k + 1)
                nc.vector.tensor_tensor(msg[:, p], ps_c[p], gate[:, p], ALU.mult).then_inc(msg_done, 1)

            def msg_low(k, p):
                dve.wait_ge(mhi_done, k + 1)
                nc.vector.tensor_tensor(m_lo[:, p], msg[:, p], m_hi[:, p].bitcast(F32), ALU.subtract).then_inc(mlo_done, 1)

            def ea_part(j):
                return ea_raw[:, j // 2, (j % 2) * 2 * P:(j % 2 + 1) * 2 * P]

            def ea_high(gc, j):
                dve.wait_ge(ea_loaded[j // 2], 16 * (gc + 1))
                nc.vector.tensor_copy(ea_st[0:DE, j, :], ea_part(j)).then_inc(ea_hi_done, 1)

            def ea_low(gc, j):
                dve.wait_ge(ea_hi_done, gc * PPG + (j + 1))
                nc.vector.tensor_tensor(ea_st[DE:2 * DE, j, :], ea_part(j), ea_st[0:DE, j, :].bitcast(F32),
                                        ALU.subtract).then_inc(ea_lo_done, 1)

            def dve_group(ps, g, first=False, last=False):
                gc = ps * GROUPS + g
                for j in range(PPG):
                    k, p = gc * PPG + j, j % 2
                    dve.wait_ge(hhi_done, k + 1)
                    nc.vector.scalar_tensor_tensor(out=h_lo[:, p], in0=ps_h[p], scalar=0.0, in1=h_hi[:, p].bitcast(F32),
                                                   op0=ALU.max, op1=ALU.subtract).then_inc(hlo_done, 1)
                    if not first:
                        dve.wait_ge(seg_done, k - 3)
                    rel = dst_rel[:, bass.ds(g * TPG + 2 * j, 2)]
                    nc.vector.tensor_tensor(sel[:, j], iota_row[:, None, :].to_broadcast([P, 2, WIN]),
                                            rel[:, :, None].to_broadcast([P, 2, WIN]), ALU.is_equal).then_inc(sel_ready, 1)
                    ahead = (gc + (j + 2) // PPG, (j + 2) % PPG) if j < 2 or not last else None
                    if ahead:
                        ea_high(*ahead)
                    if not first or j >= 2:
                        msg_low(k - 2, p)
                    if not first or j >= 1:
                        message(k - 1, (j - 1) % 2)
                    if ahead:
                        ea_low(*ahead)

            more = passes(dve)
            with dve.Fori(0, more + 1) as ps:
                pass_start(dve, ps)
                dve.wait_ge(windows_moved, ps + 1)
                nc.vector.tensor_tensor(dst_rel[:].rearrange("p (g t) -> p g t", t=TPG),
                                        dst_f[:].rearrange("p (g t) -> p g t", t=TPG),
                                        win_base[:, :, None].to_broadcast([P, GROUPS, TPG]), ALU.subtract)
                nc.vector.tensor_scalar(sum_idx[:], win_base[:], float(N), iota_part[:, 0:1], ALU.min,
                                        ALU.add).then_inc(windows_set, 1)
                dve.wait_ge(windows_set, ps + 1)
                nc.vector.tensor_scalar(win_base[:], win_base[:], float(WIN), None, ALU.add).then_inc(windows_moved, 1)
                dve.wait_ge(windows_moved, ps + 2)
                for j in range(2):
                    ea_high(ps * GROUPS, j)
                    ea_low(ps * GROUPS, j)
                dve_group(ps, 0, first=True)
                with dve.Fori(1, GROUPS - 1) as g:
                    dve_group(ps, g)
                dve_group(ps, GROUPS - 1, last=True)
                k = ps * PAIRS + PAIRS
                msg_low(k - 2, 0)
                message(k - 1, 1)
                msg_low(k - 1, 1)

            def norm_stats(c, norm):
                rows, R, _ = norm_rows(c)
                q, i = c % 2, norm_order.index((c, norm))
                for r in range(R):
                    last = nc.vector.bn_stats(n_bn[0:rows, q, r, :], n_sum[0:rows, q, r, :])
                last.then_inc(n_bn_done, 1)
                dve.wait_ge(n_bn_done, i + 1)
                for r in range(R):
                    last = nc.vector.bn_aggr(n_mv[0:rows, q, norm, r, :], n_bn[0:rows, q, r, :])
                last.then_inc(n_mv_done, 1)

            def norm_scales(c, norm):
                rows, R, _ = norm_rows(c)
                q, i = c % 2, norm_order.index((c, norm))
                dve.wait_ge(n_sd_done, i + 1)
                nc.vector.reciprocal(n_rs[0:rows, q, norm, 0:R], n_sd[0:rows, q, norm, 0:R]).then_inc(n_rs_done, 1)
                dve.wait_ge(n_rs_done, i + 1)
                nc.vector.scalar_tensor_tensor(out=n_nm[0:rows, q, norm, 0:R], in0=n_mv[0:rows, q, norm, 0:R, 0],
                                               scalar=-1.0, in1=n_rs[0:rows, q, norm, 0:R], op0=ALU.mult,
                                               op1=ALU.mult).then_inc(n_nm_done, 1)

            def norm_middle(c):
                rows, R, _ = norm_rows(c)
                q, i = c % 2, norm_order.index((c, 0))
                v = n_sum[0:rows, q, 0:R, :]
                dve.wait_ge(n_applied, i + 1)
                nc.vector.tensor_tensor(v, v, gamma_b[0:rows, None, :].to_broadcast([rows, R, H]), ALU.mult).then_inc(n_scaled, 1)
                dve.wait_ge(n_scaled, c + 1)
                dve.wait_ge(n_xb_done, c + 1)
                nc.vector.tensor_tensor(v, v, n_x[0:rows, q, 0:R, :], ALU.add).then_inc(n_mid_done, 1)
                dve.wait_ge(n_mid_done, c + 1)

            for c, norm in norm_order:
                if norm == 0:
                    dve.wait_ge(n_loaded[c % 2], 32 * (c // 2 + 1))
                else:
                    norm_middle(c)
                norm_stats(c, norm)
                norm_scales(c, norm)

        @block.gpsimd
        def _(pool):
            def waited():
                pool.sem_inc(pool_waited, 1)

            def copy_gather_idx(gc, g, h):
                if g is not None:
                    for t in range(4 * h, 4 * h + 4):
                        pool.wait_ge(gathered[t], gc * 16)
                waited()
                cols = bass.ds((0 if g is None else g) * TPG + 4 * h, 4)
                nc.gpsimd.tensor_copy(gat_idx[:, 4 * h:4 * h + 4], src_idx[:, cols]).then_inc(idx_copied, 1)
                pool.wait_ge(idx_copied, gc * 2 + (h + 1))
                waited()

            def gather(k, j, first):
                if not first:
                    pool.wait_ge(h_ready, k - 3)
                    pool.wait_ge(g_seeded, k - 3)
                    waited()
                for t in range(2 * j, 2 * j + 2):
                    nc.gpsimd.indirect_dma_start(
                        gat[:, t, :], None, node_table,
                        bass.IndirectOffsetOnAxis(ap=gat_idx[:, t:t + 1], axis=0)).then_inc(gathered[t], 16)

            def add_sum(gc, g, fresh=False):
                if not fresh:
                    pool.wait_ge(sum_added, gc * 16)
                    waited()
                nc.gpsimd.tensor_copy(sct_idx[:], sum_idx[:, bass.ds(g, 1)]).then_inc(sct_idx_copied, 1)
                pool.wait_ge(sct_idx_copied, gc + 1)
                pool.wait_ge(sum_copied, gc + 1)
                waited()
                nc.gpsimd.indirect_dma_start(
                    node_sum, bass.IndirectOffsetOnAxis(ap=sct_idx[:, 0:1], axis=0), win_sum[:], None,
                    compute_op=ALU.add).then_inc(sum_added, 16)

            def pool_group(ps, g, first=False, sums=True, fresh=False):
                gc = ps * GROUPS + g
                copy_gather_idx(gc, None if first else g, 0)
                gather(gc * PPG, 0, first)
                gather(gc * PPG + 1, 1, first)
                copy_gather_idx(gc, None if first else g, 1)
                gather(gc * PPG + 2, 2, first)
                gather(gc * PPG + 3, 3, first)
                if sums:
                    add_sum(gc - 2, g - 2, fresh)

            pool.wait_ge(indices_loaded, 16 * 5)
            pool.wait_ge(node_sum_set, 16 * 3)
            for i in range(2):
                pool.wait_ge(table_stored[i], 16 * ((NT + 1 - i) // 2))
            pool.sem_inc(pass_open, 1)
            more = passes(pool)
            with pool.Fori(0, more + 1) as ps:
                pass_start(pool, ps)
                pool.wait_ge(windows_set, ps + 1)
                pool_group(ps, 0, first=True, sums=False)
                pool_group(ps, 1, sums=False)
                pool_group(ps, 2, fresh=True)
                with pool.Fori(3, GROUPS) as g:
                    pool_group(ps, g)
                last = ps * GROUPS + (GROUPS - 1)
                add_sum(last - 1, GROUPS - 2)
                add_sum(last, GROUPS - 1)
                pool.wait_ge(sum_added, last * 16 + 16)
                pool.sem_inc(pass_open, 1)

            for c in range(NCHUNKS + 1):
                rows, R, _ = norm_rows(c)
                v = n_x[0:rows, c % 2, 0:R, :]
                pool.wait_ge(n_loaded[c % 2], 32 * (c // 2 + 1))
                nc.gpsimd.tensor_tensor(v, v, beta_b[0:rows, None, :].to_broadcast([rows, R, H]), ALU.add).then_inc(n_xb_done, 1)


def kernel(x, src, dst, edge_attr_64, L0_gnn_W1, L0_gnn_b1, L0_gnn_W2, L0_gnn_b2, L0_gnn_Wg, L0_gnn_bg,
           L0_gnn_gamma, L0_gnn_beta):
    import numpy as np
    import concourse.bacc as bacc
    from concourse import mybir as mb
    from concourse.bass_utils import run_bass_kernel_spmd

    x, src, dst, ea = (np.asarray(a) for a in (x, src, dst, edge_attr_64))
    pad = TILES * P - E
    arrays = {
        "xT": np.ascontiguousarray(x.T),
        "x": np.ascontiguousarray(x),
        "src_t": np.ascontiguousarray(np.pad(src, (0, pad)).reshape(TILES, P).T),
        "dst_t": np.ascontiguousarray(np.pad(dst, (0, pad), constant_values=-1).reshape(TILES, P).T),
        "dst": np.ascontiguousarray(dst),
        "eaT": np.ascontiguousarray(np.pad(ea, ((0, pad), (0, 0))).reshape(GROUPS, GE, DE).transpose(0, 2, 1)),
        "w1": np.ascontiguousarray(L0_gnn_W1), "b1": np.ascontiguousarray(L0_gnn_b1),
        "w2": np.ascontiguousarray(L0_gnn_W2), "b2": np.ascontiguousarray(L0_gnn_b2),
        "wg": np.ascontiguousarray(L0_gnn_Wg), "bg": np.ascontiguousarray(L0_gnn_bg),
        "gamma": np.ascontiguousarray(L0_gnn_gamma), "beta": np.ascontiguousarray(L0_gnn_beta),
        "ident_d": np.eye(P, dtype=np.float32),
        "iota_d": np.arange(P, dtype=np.float32),
    }
    nc = bacc.Bacc("TRN2", target_bir_lowering=False, num_devices=1)
    args = [nc.dram_tensor("in_" + k, a.shape, mb.dt.from_np(a.dtype), kind="ExternalInput").ap()
            for k, a in arrays.items()]
    out = nc.dram_tensor("out", (N, H), mb.dt.float32, kind="ExternalOutput").ap()
    gnn_program(nc, *args, out)
    r = run_bass_kernel_spmd(nc, [{"in_" + k: a for k, a in arrays.items()}], core_ids=[0])
    return r.results[0]["out"]
```

```python
from contextlib import ExitStack

import concourse.bass as bass
from concourse import mybir

F32 = mybir.dt.float32
F32R = mybir.dt.float32r
I32 = mybir.dt.int32
ALU = mybir.AluOpType
ACT = mybir.ActivationFunctionType
AX_X = mybir.AxisListType.X

P = 128
N, H, DE, E = 6250, 256, 64, 106250
EPS = 1e-5
TPG = 8
PPG = TPG // 2
GROUPS = -(-E // (TPG * P))
TILES = GROUPS * TPG
PAIRS = GROUPS * PPG
GE = TPG * P
HALF = GE // 2
WIN = P
SUM_ROWS = -(-(N + WIN) // P) * P
NT = -(-N // P)
XC = 7
XCHUNKS = NT // XC
XN = XC * P
NR = 3
NS = 8
TS = NS
NCHUNKS = N // (P * NR)
NREST = N - NCHUNKS * P * NR


def gnn_program(nc, xT, x, src_t, dst_t, dst, eaT, w1, b1, w2, b2, wg, bg, gamma, beta, ident_d, iota_d, out):
    assert NT == XC * XCHUNKS and 0 < NREST <= P
    node_table = nc.dram_tensor("node_table", (N, 2 * H), F32).ap()
    node_sum = nc.dram_tensor("node_sum", (SUM_ROWS, H), F32).ap()
    with ExitStack() as ctx:
        def sb(name, shape, dt=F32):
            return ctx.enter_context(nc.sbuf_tensor(name, shape, dt))

        def sem(name):
            return ctx.enter_context(nc.semaphore(name))

        bank = [ctx.enter_context(nc.psum_tensor(f"bank{i}", [P, 512], F32)) for i in range(8)]
        ps_h = [bank[i][:, :].rearrange("p (c e) -> p c e", c=2) for i in (0, 1)]
        ps_g = [bank[i][:, :].rearrange("p (t f) -> p t f", t=2) for i in (2, 3)]
        ps_c = [bank[i][:, :].rearrange("p (t f) -> p t f", t=2) for i in (4, 5)]
        ps_sum = bank[6][:, 0:H]
        ps_misc = bank[7]

        ident = sb("ident", [P, P])
        ident_r = sb("ident_r", [P, P], F32R)
        iota_row = sb("iota_row", [P, WIN])
        iota_part = sb("iota_part", [P, 1])
        ones = sb("ones", [P, P])
        wtab_raw = sb("wtab_raw", [P, 2, 2 * H])
        wtab_hi = sb("wtab_hi", [P, 2, 2 * H], F32R)
        wtab_lo = sb("wtab_lo", [P, 2, 2 * H], F32R)
        we_raw = sb("we_raw", [P, 2 * H])
        we_hi = sb("we_hi", [P, 2 * H], F32R)
        we_lo = sb("we_lo", [P, 2 * H], F32R)
        w2_raw = sb("w2_raw", [P, 2, H])
        w2_hi = sb("w2_hi", [P, 2, H], F32R)
        w2_lo = sb("w2_lo", [P, 2, H], F32R)
        b2_b = sb("b2_b", [P, 2, H])
        bias_tab = sb("bias_tab", [P, 2 * H])
        gamma_b = sb("gamma_b", [P, H])
        beta_b = sb("beta_b", [P, H])
        eps_t = sb("eps_t", [P, 1])

        src_idx = sb("src_idx", [P, TILES], I32)
        dst_i = sb("dst_i", [P, TILES], I32)
        dst_f = sb("dst_f", [P, TILES])
        dst_rel = sb("dst_rel", [P, TILES])
        grp_i = sb("grp_i", [GROUPS, GE], I32)
        grp_min = sb("grp_min", [GROUPS, 1])
        grp_max = sb("grp_max", [GROUPS, 1])
        grp_span = sb("grp_span", [GROUPS, 1])
        grp_diag = sb("grp_diag", [GROUPS, 2, GROUPS])
        win_base = sb("win_base", [P, GROUPS])
        win_clip = sb("win_clip", [P, GROUPS])
        sum_idx = sb("sum_idx", [P, GROUPS], I32)
        span_max = sb("span_max", [P, 1])
        span_int = sb("span_int", [P, 1], I32)
        more_passes = sb("more_passes", [P, 1], I32)

        gat = sb("gat", [P, TPG, 2 * H])
        gat_idx = sb("gat_idx", [P, TPG], I32)
        sct_idx = sb("sct_idx", [P, 1], I32)
        ea_raw = sb("ea_raw", [DE, 2, HALF])
        ea_st = sb("ea_st", [P, PPG, 2 * P], F32R)
        h_hi = sb("h_hi", [P, 2, 2, 2 * P], F32R)
        h_lo = sb("h_lo", [P, 2, 2, 2 * P], F32R)
        gate = sb("gate", [P, 2, 2, H])
        msg = sb("msg", [P, 2, 2, H])
        m_hi = sb("m_hi", [P, 2, 2, H], F32R)
        m_lo = sb("m_lo", [P, 2, 2, H], F32R)
        sel = sb("sel", [P, PPG, 2, WIN], F32R)
        win_sum = sb("win_sum", [P, H])

        x_raw = sb("x_raw", [P, 2, 2, XN])
        x_hi = sb("x_hi", [P, 2, 2, XN], F32R)
        x_lo = sb("x_lo", [P, 2, 2, XN], F32R)
        zero_rows = sb("zero_rows", [P, H])

        n_sum = sb("n_sum", [P, NS, NR, H])
        tab_out = n_sum[:].rearrange("p c r h -> p c (r h)")[:, :, 0:2 * H]
        n_x = sb("n_x", [P, NS, NR, H])
        n_bn = sb("n_bn", [P, 2, NR, 6])
        n_mv = sb("n_mv", [P, 2, NS, NR, 2])
        n_sd = sb("n_sd", [P, 2, NS, NR])
        n_rs = sb("n_rs", [P, 2, NS, NR])
        n_nm = sb("n_nm", [P, 2, NS, NR])

        consts_set = sem("consts_set")
        consts_loaded = sem("consts_loaded")
        scales_loaded = sem("scales_loaded")
        bias_loaded = sem("bias_loaded")
        wtab_loaded = sem("wtab_loaded")
        weights_loaded = sem("weights_loaded")
        indices_loaded = sem("indices_loaded")
        w_hi_done = sem("w_hi_done")
        w_lo_done = sem("w_lo_done")
        banks_primed = sem("banks_primed")
        stat_step = sem("stat_step")
        diag_ready = sem("diag_ready")
        stats_spread = sem("stats_spread")
        passes_known = sem("passes_known")
        windows_set = sem("windows_set")
        windows_moved = sem("windows_moved")
        x_loaded = [sem(f"x_loaded{i}") for i in range(2)]
        x_hi_done = sem("x_hi_done")
        x_lo_done = sem("x_lo_done")
        table_mm = sem("table_mm")
        table_biased = sem("table_biased")
        table_stored = [sem(f"table_stored{i}") for i in range(TS)]
        node_sum_set = sem("node_sum_set")
        ea_loaded = [sem(f"ea_loaded{i}") for i in range(2)]
        ea_hi_done = sem("ea_hi_done")
        ea_lo_done = sem("ea_lo_done")
        idx_copied = sem("idx_copied")
        gathered = [sem(f"gathered{i}") for i in range(TPG)]
        h_ready = sem("h_ready")
        g_ready = sem("g_ready")
        hhi_done = sem("hhi_done")
        hlo_done = sem("hlo_done")
        g_seeded = sem("g_seeded")
        c_seeded = sem("c_seeded")
        gate_done = sem("gate_done")
        core_ready = sem("core_ready")
        msg_done = sem("msg_done")
        mhi_done = sem("mhi_done")
        mlo_done = sem("mlo_done")
        sel_ready = sem("sel_ready")
        seg_done = sem("seg_done")
        sum_copied = sem("sum_copied")
        pool_waited = sem("pool_waited")
        sum_added = sem("sum_added")
        pass_open = sem("pass_open")
        sct_idx_copied = sem("sct_idx_copied")
        n_loaded = [sem(f"n_loaded{i}") for i in range(NS)]
        n_x_loaded = [sem(f"n_x_loaded{i}") for i in range(NS)]
        n_bn_done = [sem(f"n_bn_done{i}") for i in range(2)]
        n_mv_done = [sem(f"n_mv_done{i}") for i in range(2)]
        n_sd_done = [sem(f"n_sd_done{i}") for i in range(2)]
        n_rs_done = [sem(f"n_rs_done{i}") for i in range(2)]
        n_nm_done = [sem(f"n_nm_done{i}") for i in range(2)]
        n_applied = [sem(f"n_applied{i}") for i in range(2)]
        n_xb_done = sem("n_xb_done")
        n_scaled = sem("n_scaled")
        n_mid_done = sem("n_mid_done")
        n_stored = [sem(f"n_stored{i}") for i in range(NS)]

        xT_v = xT.rearrange("(c p) n -> p c n", c=2)
        W_LOADS = 5
        C_LOADS = 5
        STATS_AT = (10, 20, 24)
        NC = NCHUNKS + 1

        def skewed(steps):
            for n in range(NC + max(lag for _, lag in steps)):
                for step, lag in steps:
                    if 0 <= n - lag < NC:
                        step(n - lag)

        block = ctx.enter_context(nc.Block())

        def passes(eng):
            eng.wait_ge(passes_known, 1)
            return eng.value_load(more_passes[0:1, 0:1], min_val=0, max_val=N // WIN + 1)

        def pass_start(eng, ps):
            eng.wait_ge(pass_open, ps + 1)

        def x_low(eng, nc_eng, c):
            n = min(XN, N - c * XN)
            eng.wait_ge(x_hi_done, c + 1)
            nc_eng.tensor_tensor(x_lo[:, c % 2, :, 0:n], x_raw[:, c % 2, :, 0:n],
                                 x_hi[:, c % 2, :, 0:n].bitcast(F32), ALU.subtract).then_inc(x_lo_done, 1)

        def norm_rows(c):
            first = c * P * NR
            if c < NCHUNKS:
                return P, NR, slice(first, first + P * NR)
            return NREST, 1, slice(first, N)

        @block.sync
        def _(sp):
            sp.dma_start(wtab_raw[:, :, 0:H], w1[0:H, :].rearrange("(c p) f -> p c f", c=2)).then_inc(wtab_loaded, 16)
            sp.dma_start(wtab_raw[:, :, H:], wg[0:H, :].rearrange("(c p) f -> p c f", c=2)).then_inc(wtab_loaded, 16)
            sp.dma_start(x_raw[:, 0], xT_v[:, :, 0:XN]).then_inc(x_loaded[0], 16)
            sp.dma_start(x_raw[:, 1], xT_v[:, :, XN:2 * XN]).then_inc(x_loaded[1], 16)
            for k in range(2):
                sp.dma_start(we_raw[k * DE:(k + 1) * DE, 0:H], w1[H:H + DE, :]).then_inc(weights_loaded, 16)
                sp.dma_start(we_raw[k * DE:(k + 1) * DE, H:], wg[H:H + DE, :]).then_inc(weights_loaded, 16)
            sp.dma_start(w2_raw[:], w2.rearrange("(c p) f -> p c f", c=2)).then_inc(weights_loaded, 16)

            sp.dma_start(grp_i[0:GROUPS - 1, :], dst[0:(GROUPS - 1) * GE].rearrange("(g e) -> g e", e=GE)).then_inc(indices_loaded, 16)
            rest = E - (GROUPS - 1) * GE
            sp.dma_start(grp_i[GROUPS - 1:GROUPS, 0:rest], dst[(GROUPS - 1) * GE:E][None, :]).then_inc(indices_loaded, 16)
            sp.dma_start(grp_i[GROUPS - 1:GROUPS, rest:GE], dst[E - (GE - rest):E][None, :]).then_inc(indices_loaded, 16)
            sp.dma_start(dst_i[:], dst_t).then_inc(indices_loaded, 16)
            sp.dma_start(src_idx[:], src_t).then_inc(indices_loaded, 16)
            sp.dma_start(ident[:], ident_d).then_inc(consts_loaded, 16)
            sp.dma_start(iota_row[:], iota_d[None, :].to_broadcast([P, WIN])).then_inc(consts_loaded, 16)
            sp.dma_start(iota_part[:], iota_d[:, None]).then_inc(consts_loaded, 16)
            for t in range(2):
                sp.dma_start(b2_b[:, t, :], b2[None, :].to_broadcast([P, H])).then_inc(consts_loaded, 16)

            def sum_start(c):
                rows = slice(c * XN, min(N, (c + 1) * XN))
                sp.dma_start(node_sum[rows, :], x[rows, :]).then_inc(node_sum_set, 16)

            sum_start(0)
            sp.wait_ge(consts_set, 1)
            sp.dma_start(node_sum[N:N + P, :], zero_rows[:]).then_inc(node_sum_set, 16)
            sp.dma_start(node_sum[N + P:SUM_ROWS, :], zero_rows[0:SUM_ROWS - N - P, :]).then_inc(node_sum_set, 16)

            for t in range(NT):
                c, tt = t // XC, t % XC
                if tt == 2 and c + 2 < XCHUNKS:
                    n = min(XN, N - (c + 2) * XN)
                    sp.wait_ge(x_lo_done, c + 1)
                    sp.dma_start(x_raw[:, c % 2, :, 0:n],
                                 xT_v[:, :, (c + 2) * XN:(c + 2) * XN + n]).then_inc(x_loaded[c % 2], 16)
                if tt == 5 and c + 1 < XCHUNKS:
                    sum_start(c + 1)
                m = min(P, N - t * P)
                sp.wait_ge(table_biased, t + 1)
                sp.dma_start(node_table[t * P:t * P + m, :], tab_out[0:m, t % TS, :]).then_inc(table_stored[t % TS], 16)

            sp.dma_start(gamma_b[:], gamma[None, :].to_broadcast([P, H])).then_inc(scales_loaded, 16)
            sp.dma_start(beta_b[:], beta[None, :].to_broadcast([P, H])).then_inc(scales_loaded, 16)

            more = passes(sp)
            with sp.Fori(0, more + 1) as ps:
                pass_start(sp, ps)
                for h in range(2):
                    sp.dma_start(ea_raw[:, h, :], eaT[0, :, h * HALF:(h + 1) * HALF]).then_inc(ea_loaded[h], 16)
                with sp.Fori(1, GROUPS) as g:
                    for h in range(2):
                        sp.wait_ge(ea_lo_done, (ps * GROUPS + g) * PPG + (2 * h + 2 - PPG))
                        sp.dma_start(ea_raw[:, h, :], eaT[bass.ds(g, 1), :, h * HALF:(h + 1) * HALF].rearrange(
                            "o d e -> (o d) e")).then_inc(ea_loaded[h], 16)

            def load_x(c):
                q, (rows, R, at) = c % NS, norm_rows(c)
                if c >= NS:
                    sp.wait_ge(n_mid_done, c - NS + 1)
                sp.dma_start(n_x[0:rows, q, 0:R, :], x[at, :].rearrange("(p r) f -> p r f", r=R)).then_inc(n_x_loaded[q], 16)

            def load_sum(c):
                q, (rows, R, at) = c % NS, norm_rows(c)
                if c >= NS:
                    sp.wait_ge(n_stored[q], 16 * (c // NS))
                sp.dma_start(n_sum[0:rows, q, 0:R, :], node_sum[at, :].rearrange("(p r) f -> p r f", r=R)).then_inc(n_loaded[q], 16)

            def load_x_later(c):
                if c >= NS:
                    load_x(c)

            def store(c):
                q, (rows, R, at) = c % NS, norm_rows(c)
                sp.wait_ge(n_applied[1], c + 1)
                sp.dma_start(out[at, :].rearrange("(p r) f -> p r f", r=R), n_sum[0:rows, q, 0:R, :]).then_inc(n_stored[q], 16)

            sp.wait_ge(gathered[TPG - 1], (more + 1) * (16 * GROUPS))
            for c in range(NS):
                load_x(c)
            sp.wait_ge(pass_open, more + 2)
            skewed([(load_x_later, 0), (load_sum, 1), (store, NS)])
            for q in range(NS):
                sp.wait_ge(n_stored[q], 16 * ((NC + NS - 1 - q) // NS))

        @block.scalar
        def _(act):
            act.dma_start(bias_tab[:, 0:H], b1[None, :].to_broadcast([P, H])).then_inc(bias_loaded, 16)
            act.dma_start(bias_tab[:, H:], bg[None, :].to_broadcast([P, H])).then_inc(bias_loaded, 16)
            act.wait_ge(wtab_loaded, 16 * 2)
            nc.scalar.activation(wtab_hi[:], wtab_raw[:], ACT.Copy).then_inc(w_hi_done, 1)

            for c in range(XCHUNKS):
                n = min(XN, N - c * XN)
                act.wait_ge(x_loaded[c % 2], 16 * (c // 2 + 1))
                if c >= 2:
                    act.wait_ge(table_mm, (c - 1) * XC)
                nc.scalar.activation(x_hi[:, c % 2, :, 0:n], x_raw[:, c % 2, :, 0:n], ACT.Copy).then_inc(x_hi_done, 1)
                if c == 1:
                    act.wait_ge(weights_loaded, 16 * W_LOADS)
                    nc.scalar.activation(we_hi[:], we_raw[:], ACT.Copy).then_inc(w_hi_done, 1)
                    nc.scalar.activation(w2_hi[:], w2_raw[:], ACT.Copy).then_inc(w_hi_done, 1)

            def seed_gate(gc, j):
                for t in (2 * j, 2 * j + 1):
                    act.wait_ge(gathered[t], 16 * (gc + 1))
                nc.scalar.activation(ps_g[j % 2], gat[:, 2 * j:2 * j + 2, H:], ACT.Copy).then_inc(g_seeded, 1)

            def seed_core(j):
                nc.scalar.activation(ps_c[j % 2], b2_b[:], ACT.Copy).then_inc(c_seeded, 1)

            def msg_high(k, p):
                act.wait_ge(msg_done, k + 1)
                nc.scalar.activation(m_hi[:, p], msg[:, p], ACT.Copy).then_inc(mhi_done, 1)

            def copy_sum(gc, fresh=False):
                act.wait_ge(seg_done, gc * PPG + PPG)
                if not fresh:
                    act.wait_ge(sum_added, gc * 16)
                nc.scalar.activation(win_sum[:], ps_sum, ACT.Copy).then_inc(sum_copied, 1)

            def act_group(ps, g, first=False, last=False, second=False):
                gc = ps * GROUPS + g
                for j in range(PPG):
                    k, p = gc * PPG + j, j % 2
                    if j == PPG - 1 and not first:
                        copy_sum(gc - 1, second)
                    act.wait_ge(h_ready, k + 1)
                    if not first or j >= 2:
                        act.wait_ge(core_ready, k - 1)
                    nc.scalar.activation(h_hi[:, p], ps_h[p], ACT.Relu).then_inc(hhi_done, 1)
                    if not first or j >= 2:
                        if not first:
                            act.wait_ge(seg_done, k - 3)
                        msg_high(k - 2, p)
                    act.wait_ge(g_ready, k + 1)
                    if not first or j >= 2:
                        act.wait_ge(msg_done, k - 1)
                    nc.scalar.activation(gate[:, p], ps_g[p], ACT.Sigmoid).then_inc(gate_done, 1)
                    if not last or j < PPG - 1:
                        if not first or j >= 1:
                            act.wait_ge(gate_done, k)
                        seed_gate(gc + (j + 1) // PPG, (j + 1) % PPG)
                    seed_core(j)

            act.wait_ge(banks_primed, 1)
            more = passes(act)
            with act.Fori(0, more + 1) as ps:
                pass_start(act, ps)
                seed_gate(ps * GROUPS, 0)
                act_group(ps, 0, first=True)
                act_group(ps, 1, second=True)
                with act.Fori(2, GROUPS - 1) as g:
                    act_group(ps, g)
                act_group(ps, GROUPS - 1, last=True)
                k = ps * PAIRS + PAIRS
                for p in range(2):
                    act.wait_ge(seg_done, k - 3 + p)
                    msg_high(k - 2 + p, p)
                copy_sum(ps * GROUPS + (GROUPS - 1))

            def deviation(norm):
                def step(c):
                    rows, R, _ = norm_rows(c)
                    act.wait_ge(n_mv_done[norm], c + 1)
                    nc.scalar.activation(n_sd[0:rows, norm, c % NS, 0:R], n_mv[0:rows, norm, c % NS, 0:R, 1], ACT.Sqrt,
                                         bias=eps_t[0:rows, :]).then_inc(n_sd_done[norm], 1)
                return step

            def apply(norm):
                def step(c):
                    rows, R, _ = norm_rows(c)
                    q = c % NS
                    act.wait_ge(n_nm_done[norm], c + 1)
                    for r in range(R):
                        last = nc.scalar.activation(n_sum[0:rows, q, r, :], n_sum[0:rows, q, r, :], ACT.Identity,
                                                    scale=n_rs[0:rows, norm, q, r:r + 1], bias=n_nm[0:rows, norm, q, r:r + 1])
                    last.then_inc(n_applied[norm], 1)
                return step

            skewed([(deviation(0), 0), (apply(0), 0), (deviation(1), 2), (apply(1), 3)])

        @block.tensor
        def _(pe):
            pe.wait_ge(w_lo_done, 1)
            for i in (2, 3, 4, 5):
                mm = nc.tensor.matmul(bank[i][:, :], wtab_hi[:, 0, 0:P], wtab_hi[:, 1, :], start=True, stop=True)
            mm.then_inc(banks_primed, 1)

            for t in range(NT):
                c, tt = t // XC, t % XC
                m = min(P, N - t * P)
                if t == STATS_AT[1]:
                    pe.wait_ge(consts_set, 2)
                    pe.wait_ge(diag_ready, 1)
                    nc.tensor.matmul(ps_misc[:, 0:2 * GROUPS], ones[0:GROUPS, :],
                                     grp_diag[:].rearrange("g a b -> g (a b)"), start=True, stop=True).then_inc(stats_spread, 1)
                if tt == 0:
                    pe.wait_ge(x_lo_done, c + 1)
                if t >= 2:
                    pe.wait_ge(table_biased, t - 1)
                terms = [(a, b, k) for k in range(2) for a, b in ((x_hi, wtab_hi), (x_hi, wtab_lo), (x_lo, wtab_hi))]
                for i, (a, b, k) in enumerate(terms):
                    mm = nc.tensor.matmul(bank[t % 2][0:m, :], a[:, c % 2, k, tt * P:tt * P + m], b[:, k, :],
                                          start=(i == 0), stop=(i == len(terms) - 1))
                mm.then_inc(table_mm, 1)

            def transpose_gathered(k, gc, pairs, first):
                if not first or pairs[0] >= 2:
                    pe.wait_ge(hlo_done, k)
                for i in pairs:
                    for t in range(2):
                        pe.wait_ge(gathered[2 * i + t], 16 * (gc + 1))
                        for c in range(2):
                            nc.tensor.matmul(ps_h[i % 2][:, c, t * P:(t + 1) * P].bitcast(F32R),
                                             gat[:, 2 * i + t, c * P:(c + 1) * P].bitcast(F32R), ident_r[:],
                                             start=(t == 0 and c == 0), stop=False, is_transpose=True,
                                             skip_group_check=True)

            def front(k, gc, j):
                p = j % 2
                pe.wait_ge(ea_lo_done, k + 1)
                ea = ea_st[:, j, :]
                for c in range(2):
                    for w in (we_hi, we_lo):
                        mm = nc.tensor.matmul(ps_h[p][:, c, :], w[:, c * P:(c + 1) * P], ea, start=False,
                                              stop=(c == 1 and w is we_lo), skip_group_check=True)
                mm.then_inc(h_ready, 1)
                pe.wait_ge(g_seeded, k + 1)
                for t in range(2):
                    for w in (we_hi, we_lo):
                        mm = nc.tensor.matmul(ps_g[p][:, t, :], ea[:, t * P:(t + 1) * P], w[:, H:],
                                              start=False, stop=(w is we_lo), skip_group_check=True)
                mm.then_inc(g_ready, 1)

            def core(k, j):
                p = j % 2
                pe.wait_ge(c_seeded, k + 1)
                pe.wait_ge(hlo_done, k + 1)
                for t in range(2):
                    terms = [(a, b, c) for c in range(2) for a, b in ((h_hi, w2_hi), (h_hi, w2_lo), (h_lo, w2_hi))]
                    for i, (a, b, c) in enumerate(terms):
                        mm = nc.tensor.matmul(ps_c[p][:, t, :], a[:, p, c, t * P:(t + 1) * P], b[:, c, :],
                                              start=False, stop=(t == 1 and i == len(terms) - 1),
                                              skip_group_check=True)
                mm.then_inc(core_ready, 1)

            def segment(k, gc, j, first=False):
                p = j % 2
                if j == 0 and not first:
                    pe.wait_ge(sum_copied, gc)
                pe.wait_ge(sel_ready, k + 1)
                pe.wait_ge(mlo_done, k + 1)
                for t in range(2):
                    for m in (m_hi, m_lo):
                        mm = nc.tensor.matmul(ps_sum, sel[:, j, t, :], m[:, p, t, :],
                                              start=(j == 0 and t == 0 and m is m_hi),
                                              stop=(j == PPG - 1 and t == 1 and m is m_lo))
                mm.then_inc(seg_done, 1)

            def pe_group(ps, g, first=False):
                gc = ps * GROUPS + g
                for j in range(PPG):
                    k = gc * PPG + j
                    if first and j < 2:
                        transpose_gathered(k, gc, (j,), first)
                    elif j % 2 == 0:
                        transpose_gathered(k, gc, (j, j + 1), first)
                    front(k, gc, j)
                    if not first or j >= 1:
                        core(k - 1, (j - 1) % PPG)
                    if not first or j >= 3:
                        segment(k - 3, gc if j >= 3 else gc - 1, (j - 3) % PPG, first)

            pe.wait_ge(w_lo_done, 3)
            more = passes(pe)
            with pe.Fori(0, more + 1) as ps:
                pass_start(pe, ps)
                pe_group(ps, 0, first=True)
                with pe.Fori(1, GROUPS) as g:
                    pe_group(ps, g)
                gc = ps * GROUPS + (GROUPS - 1)
                k = gc * PPG + PPG
                core(k - 1, PPG - 1)
                for j in range(1, PPG):
                    segment(gc * PPG + j, gc, j)

        @block.vector
        def _(dve):
            nc.vector.memset(zero_rows[:], 0.0).then_inc(consts_set, 1)
            nc.vector.memset(ones[:], 1.0).then_inc(consts_set, 1)
            nc.vector.memset(eps_t[:], EPS)

            dve.wait_ge(w_hi_done, 1)
            nc.vector.tensor_tensor(wtab_lo[:], wtab_raw[:], wtab_hi[:].bitcast(F32), ALU.subtract).then_inc(w_lo_done, 1)
            x_low(dve, nc.vector, 0)

            dve.wait_ge(bias_loaded, 16 * 2)
            for t in range(NT):
                m = min(P, N - t * P)
                if t == STATS_AT[0]:
                    dve.wait_ge(indices_loaded, 16 * 5)
                    dve.wait_ge(consts_loaded, 16 * C_LOADS)
                    nc.vector.tensor_copy(ident_r[:], ident[:])
                    nc.vector.tensor_copy(dst_f[:], dst_i[:])
                    nc.vector.tensor_reduce(grp_min[:], grp_i[:], AX_X, ALU.min)
                if t == STATS_AT[0] + 2:
                    nc.vector.tensor_reduce(grp_max[:], grp_i[:], AX_X, ALU.max).then_inc(stat_step, 1)
                    dve.wait_ge(stat_step, 1)
                    nc.vector.tensor_tensor(grp_span[:], grp_max[:], grp_min[:], ALU.subtract).then_inc(stat_step, 1)
                    dve.wait_ge(stat_step, 2)
                    nc.vector.tensor_scalar(grp_diag[:, 0, :], ident[0:GROUPS, 0:GROUPS], grp_min[:, 0:1], None, ALU.mult)
                    nc.vector.tensor_scalar(grp_diag[:, 1, :], ident[0:GROUPS, 0:GROUPS], grp_span[:, 0:1], None,
                                            ALU.mult).then_inc(diag_ready, 1)
                if t == STATS_AT[2]:
                    dve.wait_ge(stats_spread, 1)
                    nc.vector.tensor_copy(win_base[:], ps_misc[:, 0:GROUPS]).then_inc(windows_moved, 1)
                    nc.vector.tensor_reduce(span_max[:], ps_misc[:, GROUPS:2 * GROUPS], AX_X, ALU.max).then_inc(stat_step, 1)
                    dve.wait_ge(stat_step, 3)
                    nc.vector.tensor_copy(span_int[:], span_max[:]).then_inc(stat_step, 1)
                    dve.wait_ge(stat_step, 4)
                    nc.vector.tensor_scalar(more_passes[:], span_int[:], WIN.bit_length() - 1, None,
                                            ALU.arith_shift_right).then_inc(passes_known, 1)
                if t == STATS_AT[2] + 2:
                    dve.wait_ge(w_hi_done, 3)
                    nc.vector.tensor_tensor(we_lo[:], we_raw[:], we_hi[:].bitcast(F32), ALU.subtract).then_inc(w_lo_done, 1)
                    nc.vector.tensor_tensor(w2_lo[:], w2_raw[:], w2_hi[:].bitcast(F32), ALU.subtract).then_inc(w_lo_done, 1)
                dve.wait_ge(table_mm, t + 1)
                if t >= TS:
                    dve.wait_ge(table_stored[t % TS], 16 * (t // TS))
                nc.vector.tensor_tensor(tab_out[0:m, t % TS, :], bank[t % 2][0:m, :], bias_tab[0:m, :],
                                        ALU.add).then_inc(table_biased, 1)

            def message(k, p):
                dve.wait_ge(core_ready, k + 1)
                dve.wait_ge(gate_done, k + 1)
                nc.vector.tensor_tensor(msg[:, p], ps_c[p], gate[:, p], ALU.mult).then_inc(msg_done, 1)

            def msg_low(k, p):
                dve.wait_ge(mhi_done, k + 1)
                nc.vector.tensor_tensor(m_lo[:, p], msg[:, p], m_hi[:, p].bitcast(F32), ALU.subtract).then_inc(mlo_done, 1)

            def ea_part(j):
                return ea_raw[:, j // 2, (j % 2) * 2 * P:(j % 2 + 1) * 2 * P]

            def ea_high(gc, j):
                dve.wait_ge(ea_loaded[j // 2], 16 * (gc + 1))
                nc.vector.tensor_copy(ea_st[0:DE, j, :], ea_part(j)).then_inc(ea_hi_done, 1)

            def ea_low(gc, j):
                dve.wait_ge(ea_hi_done, gc * PPG + (j + 1))
                nc.vector.tensor_tensor(ea_st[DE:2 * DE, j, :], ea_part(j), ea_st[0:DE, j, :].bitcast(F32),
                                        ALU.subtract).then_inc(ea_lo_done, 1)

            def dve_group(ps, g, first=False, last=False):
                gc = ps * GROUPS + g
                for j in range(PPG):
                    k, p = gc * PPG + j, j % 2
                    dve.wait_ge(hhi_done, k + 1)
                    nc.vector.scalar_tensor_tensor(out=h_lo[:, p], in0=ps_h[p], scalar=0.0, in1=h_hi[:, p].bitcast(F32),
                                                   op0=ALU.max, op1=ALU.subtract).then_inc(hlo_done, 1)
                    if not first:
                        dve.wait_ge(seg_done, k - 3)
                    rel = dst_rel[:, bass.ds(g * TPG + 2 * j, 2)]
                    nc.vector.tensor_tensor(sel[:, j], iota_row[:, None, :].to_broadcast([P, 2, WIN]),
                                            rel[:, :, None].to_broadcast([P, 2, WIN]), ALU.is_equal).then_inc(sel_ready, 1)
                    ahead = (gc + (j + 2) // PPG, (j + 2) % PPG) if j < 2 or not last else None
                    if ahead:
                        ea_high(*ahead)
                    if not first or j >= 2:
                        msg_low(k - 2, p)
                    if not first or j >= 1:
                        message(k - 1, (j - 1) % 2)
                    if ahead:
                        ea_low(*ahead)

            more = passes(dve)
            with dve.Fori(0, more + 1) as ps:
                pass_start(dve, ps)
                dve.wait_ge(windows_moved, ps + 1)
                nc.vector.tensor_tensor(dst_rel[:].rearrange("p (g t) -> p g t", t=TPG),
                                        dst_f[:].rearrange("p (g t) -> p g t", t=TPG),
                                        win_base[:, :, None].to_broadcast([P, GROUPS, TPG]), ALU.subtract)
                nc.vector.tensor_scalar(sum_idx[:], win_base[:], float(N), iota_part[:, 0:1], ALU.min,
                                        ALU.add).then_inc(windows_set, 1)
                dve.wait_ge(windows_set, ps + 1)
                nc.vector.tensor_scalar(win_base[:], win_base[:], float(WIN), None, ALU.add).then_inc(windows_moved, 1)
                dve.wait_ge(windows_moved, ps + 2)
                for j in range(2):
                    ea_high(ps * GROUPS, j)
                    ea_low(ps * GROUPS, j)
                dve_group(ps, 0, first=True)
                with dve.Fori(1, GROUPS - 1) as g:
                    dve_group(ps, g)
                dve_group(ps, GROUPS - 1, last=True)
                k = ps * PAIRS + PAIRS
                msg_low(k - 2, 0)
                message(k - 1, 1)
                msg_low(k - 1, 1)

            def moments(norm):
                def step(c):
                    rows, R, _ = norm_rows(c)
                    q = c % NS
                    if norm == 0:
                        dve.wait_ge(n_loaded[q], 16 * (c // NS + 1))
                    else:
                        dve.wait_ge(n_mid_done, c + 1)
                    for r in range(R):
                        last = nc.vector.bn_stats(n_bn[0:rows, norm, r, :], n_sum[0:rows, q, r, :])
                    last.then_inc(n_bn_done[norm], 1)
                return step

            def mean_var(norm):
                def step(c):
                    rows, R, _ = norm_rows(c)
                    dve.wait_ge(n_bn_done[norm], c + 1)
                    for r in range(R):
                        last = nc.vector.bn_aggr(n_mv[0:rows, norm, c % NS, r, :], n_bn[0:rows, norm, r, :])
                    last.then_inc(n_mv_done[norm], 1)
                return step

            def inverse(norm):
                def step(c):
                    rows, R, _ = norm_rows(c)
                    dve.wait_ge(n_sd_done[norm], c + 1)
                    nc.vector.reciprocal(n_rs[0:rows, norm, c % NS, 0:R],
                                         n_sd[0:rows, norm, c % NS, 0:R]).then_inc(n_rs_done[norm], 1)
                return step

            def shift(norm):
                def step(c):
                    rows, R, _ = norm_rows(c)
                    dve.wait_ge(n_rs_done[norm], c + 1)
                    nc.vector.scalar_tensor_tensor(
                        out=n_nm[0:rows, norm, c % NS, 0:R], in0=n_mv[0:rows, norm, c % NS, 0:R, 0], scalar=-1.0,
                        in1=n_rs[0:rows, norm, c % NS, 0:R], op0=ALU.mult, op1=ALU.mult).then_inc(n_nm_done[norm], 1)
                return step

            def middle(c):
                rows, R, _ = norm_rows(c)
                v = n_sum[0:rows, c % NS, 0:R, :]
                dve.wait_ge(n_scaled, c + 1)
                nc.vector.tensor_tensor(v, v, n_x[0:rows, c % NS, 0:R, :], ALU.add).then_inc(n_mid_done, 1)

            skewed([(moments(0), 0), (middle, 2), (mean_var(0), 0), (inverse(1), 3), (moments(1), 2), (shift(1), 3),
                    (mean_var(1), 2), (inverse(0), 0), (shift(0), 0)])

        @block.gpsimd
        def _(pool):
            def waited():
                pool.sem_inc(pool_waited, 1)

            def copy_gather_idx(gc, g, h):
                if g is not None:
                    for t in range(4 * h, 4 * h + 4):
                        pool.wait_ge(gathered[t], gc * 16)
                waited()
                cols = bass.ds((0 if g is None else g) * TPG + 4 * h, 4)
                nc.gpsimd.tensor_copy(gat_idx[:, 4 * h:4 * h + 4], src_idx[:, cols]).then_inc(idx_copied, 1)
                pool.wait_ge(idx_copied, gc * 2 + (h + 1))
                waited()

            def gather(k, j, first):
                if not first:
                    pool.wait_ge(h_ready, k - 3)
                    pool.wait_ge(g_seeded, k - 3)
                    waited()
                for t in range(2 * j, 2 * j + 2):
                    nc.gpsimd.indirect_dma_start(
                        gat[:, t, :], None, node_table,
                        bass.IndirectOffsetOnAxis(ap=gat_idx[:, t:t + 1], axis=0)).then_inc(gathered[t], 16)

            def add_sum(gc, g, fresh=False):
                if fresh:
                    pool.wait_ge(node_sum_set, 16 * (XCHUNKS + 2))
                else:
                    pool.wait_ge(sum_added, gc * 16)
                    waited()
                nc.gpsimd.tensor_copy(sct_idx[:], sum_idx[:, bass.ds(g, 1)]).then_inc(sct_idx_copied, 1)
                pool.wait_ge(sct_idx_copied, gc + 1)
                pool.wait_ge(sum_copied, gc + 1)
                waited()
                nc.gpsimd.indirect_dma_start(
                    node_sum, bass.IndirectOffsetOnAxis(ap=sct_idx[:, 0:1], axis=0), win_sum[:], None,
                    compute_op=ALU.add).then_inc(sum_added, 16)

            def pool_group(ps, g, first=False, sums=True, fresh=False):
                gc = ps * GROUPS + g
                copy_gather_idx(gc, None if first else g, 0)
                if first:
                    for i in range(TS):
                        pool.wait_ge(table_stored[i], 16 * ((NT + TS - 1 - i) // TS))
                    waited()
                gather(gc * PPG, 0, first)
                gather(gc * PPG + 1, 1, first)
                copy_gather_idx(gc, None if first else g, 1)
                gather(gc * PPG + 2, 2, first)
                gather(gc * PPG + 3, 3, first)
                if sums:
                    add_sum(gc - 2, g - 2, fresh)

            pool.wait_ge(x_lo_done, 1)
            for c in range(1, XCHUNKS):
                if c >= 2:
                    pool.wait_ge(table_mm, (c - 1) * XC)
                x_low(pool, nc.gpsimd, c)

            pool.sem_inc(pass_open, 1)
            pool.wait_ge(indices_loaded, 16 * 5)
            more = passes(pool)
            with pool.Fori(0, more + 1) as ps:
                pass_start(pool, ps)
                pool.wait_ge(windows_set, ps + 1)
                pool_group(ps, 0, first=True, sums=False)
                pool_group(ps, 1, sums=False)
                pool_group(ps, 2, fresh=True)
                with pool.Fori(3, GROUPS) as g:
                    pool_group(ps, g)
                last = ps * GROUPS + (GROUPS - 1)
                add_sum(last - 1, GROUPS - 2)
                add_sum(last, GROUPS - 1)
                pool.wait_ge(sum_added, last * 16 + 16)
                pool.sem_inc(pass_open, 1)

            def add_beta(c):
                rows, R, _ = norm_rows(c)
                v = n_x[0:rows, c % NS, 0:R, :]
                pool.wait_ge(n_x_loaded[c % NS], 16 * (c // NS + 1))
                nc.gpsimd.tensor_tensor(v, v, beta_b[0:rows, None, :].to_broadcast([rows, R, H]), ALU.add).then_inc(n_xb_done, 1)

            def scale_gamma(c):
                rows, R, _ = norm_rows(c)
                v = n_sum[0:rows, c % NS, 0:R, :]
                pool.wait_ge(n_applied[0], c + 1)
                nc.gpsimd.tensor_tensor(v, v, gamma_b[0:rows, None, :].to_broadcast([rows, R, H]), ALU.mult).then_inc(n_scaled, 1)

            pool.wait_ge(scales_loaded, 16 * 2)
            skewed([(add_beta, 0), (scale_gamma, 1)])


def kernel(x, src, dst, edge_attr_64, L0_gnn_W1, L0_gnn_b1, L0_gnn_W2, L0_gnn_b2, L0_gnn_Wg, L0_gnn_bg,
           L0_gnn_gamma, L0_gnn_beta):
    import numpy as np
    import concourse.bacc as bacc
    from concourse import mybir as mb
    from concourse.bass_utils import run_bass_kernel_spmd

    x, src, dst, ea = (np.asarray(a) for a in (x, src, dst, edge_attr_64))
    pad = TILES * P - E
    arrays = {
        "xT": np.ascontiguousarray(x.T),
        "x": np.ascontiguousarray(x),
        "src_t": np.ascontiguousarray(np.pad(src, (0, pad)).reshape(TILES, P).T),
        "dst_t": np.ascontiguousarray(np.pad(dst, (0, pad), constant_values=-1).reshape(TILES, P).T),
        "dst": np.ascontiguousarray(dst),
        "eaT": np.ascontiguousarray(np.pad(ea, ((0, pad), (0, 0))).reshape(GROUPS, GE, DE).transpose(0, 2, 1)),
        "w1": np.ascontiguousarray(L0_gnn_W1), "b1": np.ascontiguousarray(L0_gnn_b1),
        "w2": np.ascontiguousarray(L0_gnn_W2), "b2": np.ascontiguousarray(L0_gnn_b2),
        "wg": np.ascontiguousarray(L0_gnn_Wg), "bg": np.ascontiguousarray(L0_gnn_bg),
        "gamma": np.ascontiguousarray(L0_gnn_gamma), "beta": np.ascontiguousarray(L0_gnn_beta),
        "ident_d": np.eye(P, dtype=np.float32),
        "iota_d": np.arange(P, dtype=np.float32),
    }
    nc = bacc.Bacc("TRN2", target_bir_lowering=False, num_devices=1)
    args = [nc.dram_tensor("in_" + k, a.shape, mb.dt.from_np(a.dtype), kind="ExternalInput").ap()
            for k, a in arrays.items()]
    out = nc.dram_tensor("out", (N, H), mb.dt.float32, kind="ExternalOutput").ap()
    gnn_program(nc, *args, out)
    r = run_bass_kernel_spmd(nc, [{"in_" + k: a for k, a in arrays.items()}], core_ids=[0])
    return r.results[0]["out"]
```
